# Optimizing a Trainium2 kernel written in Bass

```python
import numpy as np
import jax
import jax.numpy as jnp

def _softmax(x, axis=-1):
    return jax.nn.softmax(x, axis=axis)

def _gelu(x):
    return jax.nn.gelu(x, approximate=True)

def _silu(x):
    return jax.nn.silu(x)

def _sigmoid(x):
    return jax.nn.sigmoid(x)

def _layernorm(x, axis=-1, eps=1e-05):
    m = jnp.mean(x, axis=axis, keepdims=True)
    v = jnp.var(x, axis=axis, keepdims=True)
    return (x - m) / jnp.sqrt(v + eps)

def _scatter_add(tgt, idx, src, axis=0):
    return tgt.at[idx].add(src)

def _segment_sum(src, seg, n):
    return jax.ops.segment_sum(src, seg, n)
kernel_name = 'mk_macaron_d1_jaxref_r4_f21ebb'

def setup_inputs(seed: int=0):
    np.random.seed(seed)
    _w = jnp.asarray

    def _L0_attn_setup():
        import math
        import jax, jax.numpy as jnp
        import numpy as np
        K_TOP = 8
        D_HEAD = 32

        def causal_topk_adjacency(x, K):
            B, T, D = x.shape
            sim = jnp.einsum('btd,bsd->bts', x, x) / math.sqrt(D)
            causal = jnp.tril(jnp.ones((T, T), dtype=bool), k=-1)
            neg = jnp.finfo(sim.dtype).min
            sim_m = jnp.where(causal[None], sim, neg)
            vals, idx = jax.lax.top_k(sim_m, K)
            valid = (vals > neg).astype(x.dtype)
            b = jnp.arange(B)[:, None, None]
            t = jnp.arange(T)[None, :, None]
            A = jnp.zeros((B, T, T), x.dtype).at[b, t, idx].max(valid)
            return A
        key = jax.random.key(seed)
        ks = jax.random.split(key, 3)
        B, T, D = (2, 1024, 256)
        x = jax.random.normal(ks[0], (B, T, D), dtype=jnp.float32)
        W_q = jax.random.normal(ks[1], (D_HEAD, D), dtype=jnp.float32) * (1.0 / math.sqrt(D))
        W_k = jax.random.normal(ks[2], (D_HEAD, D), dtype=jnp.float32) * (1.0 / math.sqrt(D))
        gain = jnp.ones((D,), dtype=jnp.float32)
        bias = jnp.zeros((D,), dtype=jnp.float32)
        log_mix = jnp.zeros((), dtype=jnp.float32)
        log_scale = jnp.zeros((), dtype=jnp.float32)
        return {'x': x, 'W_q': W_q, 'W_k': W_k, 'gain': gain, 'bias': bias, 'log_mix': log_mix, 'log_scale': log_scale}
    _L0_attn_in = _L0_attn_setup()

    def _L0_ffn_setup():
        import jax, jax.numpy as jnp
        import numpy as np
        DIM = 256
        N_EXPERTS = 8
        D_FF = 512
        TOP_K = 2
        key = jax.random.key(seed)
        ks = jax.random.split(key, 5)
        s = 0.02
        return {'x': jax.random.normal(ks[0], (2, 512, DIM), dtype=jnp.float32), 'gate_w': jax.random.normal(ks[1], (N_EXPERTS, DIM), dtype=jnp.float32) * s, 'w1': jax.random.normal(ks[2], (N_EXPERTS, D_FF, DIM), dtype=jnp.float32) * s, 'w2': jax.random.normal(ks[3], (N_EXPERTS, DIM, D_FF), dtype=jnp.float32) * s, 'w3': jax.random.normal(ks[4], (N_EXPERTS, D_FF, DIM), dtype=jnp.float32) * s}
    _L0_ffn_in = _L0_ffn_setup()
    _d = {'L0_attn_x': _L0_attn_in['x'], 'L0_attn_W_q': _L0_attn_in['W_q'], 'L0_attn_W_k': _L0_attn_in['W_k'], 'L0_attn_gain': _L0_attn_in['gain'], 'L0_attn_bias': _L0_attn_in['bias'], 'L0_attn_log_mix': _L0_attn_in['log_mix'], 'L0_attn_log_scale': _L0_attn_in['log_scale'], 'L0_ffn_gate_w': _L0_ffn_in['gate_w'], 'L0_ffn_w1': _L0_ffn_in['w1'], 'L0_ffn_w2': _L0_ffn_in['w2'], 'L0_ffn_w3': _L0_ffn_in['w3']}
    _x0 = _d['L0_attn_x']
    _d['L0_attn_x'] = jax.random.normal(jax.random.fold_in(jax.random.key(seed), 1), (8, 512, 256), dtype=_x0.dtype)
    del _x0
    return _d

def reference(L0_attn_x, L0_attn_W_q, L0_attn_W_k, L0_attn_gain, L0_attn_bias, L0_attn_log_mix, L0_attn_log_scale, L0_ffn_gate_w, L0_ffn_w1, L0_ffn_w2, L0_ffn_w3):

    def _L0_attn_ref(x, W_q, W_k, gain, bias, log_mix, log_scale):
        import math
        import jax, jax.numpy as jnp
        import numpy as np
        K_TOP = 8
        D_HEAD = 32

        def causal_topk_adjacency(x, K):
            B, T, D = x.shape
            sim = jnp.einsum('btd,bsd->bts', x, x) / math.sqrt(D)
            causal = jnp.tril(jnp.ones((T, T), dtype=bool), k=-1)
            neg = jnp.finfo(sim.dtype).min
            sim_m = jnp.where(causal[None], sim, neg)
            vals, idx = jax.lax.top_k(sim_m, K)
            valid = (vals > neg).astype(x.dtype)
            b = jnp.arange(B)[:, None, None]
            t = jnp.arange(T)[None, :, None]
            A = jnp.zeros((B, T, T), x.dtype).at[b, t, idx].max(valid)
            return A
        B, T, D = x.shape
        mix = jax.nn.sigmoid(log_mix)
        scale = jax.nn.softplus(log_scale) + 0.01
        A = causal_topk_adjacency(x, K_TOP)
        q = jnp.einsum('btd,hd->bth', x, W_q)
        k = jnp.einsum('bsd,hd->bsh', x, W_k)
        score = jnp.einsum('bth,bsh->bts', q, k) / math.sqrt(D_HEAD)
        score = jnp.where(A < 0.5, -1000000000.0, score)
        row_max = jax.lax.stop_gradient(jnp.max(score, axis=-1, keepdims=True))
        score = score - row_max
        attn = jax.nn.softmax(score, axis=-1)
        attn = jnp.nan_to_num(attn, nan=0.0)
        msg = jnp.einsum('bts,bsd->btd', attn, x)
        blended = mix * x + (1.0 - mix) * msg
        delta = jax.nn.gelu(blended * gain + bias, approximate=False) * scale
        return delta

    def _L0_ffn_ref(x, gate_w, w1, w2, w3):
        import jax, jax.numpy as jnp
        import numpy as np
        DIM = 256
        N_EXPERTS = 8
        D_FF = 512
        TOP_K = 2
        orig_shape = x.shape
        xf = x.reshape(-1, orig_shape[-1])
        scores = jnp.einsum('td,ed->te', xf, gate_w)
        probs = jax.nn.softmax(scores.astype(jnp.float32), axis=-1)
        weights, idx = jax.lax.top_k(probs, TOP_K)
        weights = weights / jnp.sum(weights, axis=-1, keepdims=True)
        weights = weights.astype(x.dtype)
        x1 = jax.nn.silu(jnp.einsum('td,efd->tef', xf, w1))
        x3 = jnp.einsum('td,efd->tef', xf, w3)
        out_all = jnp.einsum('tef,edf->ted', x1 * x3, w2)
        expert_outs = jnp.take_along_axis(out_all, idx[:, :, None], axis=1)
        result = jnp.einsum('tkd,tk->td', expert_outs, weights)
        return result.reshape(orig_shape)
    x = L0_attn_x
    x = x + 0.5 * _L0_ffn_ref(_layernorm(x, axis=-1), L0_ffn_gate_w, L0_ffn_w1, L0_ffn_w2, L0_ffn_w3)
    x = x + _L0_attn_ref(_layernorm(x, axis=-1), L0_attn_W_q, L0_attn_W_k, L0_attn_gain, L0_attn_bias, L0_attn_log_mix, L0_attn_log_scale)
    x = x + 0.5 * _L0_ffn_ref(_layernorm(x, axis=-1), L0_ffn_gate_w, L0_ffn_w1, L0_ffn_w2, L0_ffn_w3)
    return x

_drawn_inputs = setup_inputs


def setup_inputs(seed=0):
    import zlib

    import numpy as np

    out = dict(_drawn_inputs(seed))
    spreads = {'L0_attn_gain': (1.0, 0.2), 'L0_attn_bias': (0.0, 0.1)}
    factors = {'L0_ffn_gate_w': 3.228, 'L0_ffn_w1': 2.873, 'L0_ffn_w2': 2.877, 'L0_ffn_w3': 2.881}
    for name, (base, spread) in spreads.items():
        noise = np.random.default_rng([zlib.crc32(name.encode()), seed]).standard_normal(out[name].shape)
        drawn = base * np.exp(spread * noise) if base else spread * noise
        out[name] = jnp.asarray(drawn.astype(out[name].dtype))
    for name, factor in factors.items():
        out[name] = (out[name] * factor).astype(out[name].dtype)
    return out
```

```python
from contextlib import ExitStack

import concourse.bass as bass
from concourse import mybir

ALU = mybir.AluOpType
ACT = mybir.ActivationFunctionType
AX = mybir.AxisListType
F32 = mybir.dt.float32
F16 = mybir.dt.float16
BF16 = mybir.dt.bfloat16
I32 = mybir.dt.int32

T = 4096
D = 256
NE = 8
NT = T // 128
C = 2
NTC = NT // C
CAP = NTC * 128 + 128
NJ = 2 * NTC + NE - 1
SPARE = NE * CAP
ROWS = SPARE + 128
W2OFF = 16 * 2048
NEG = -(2.0 ** 100)
MARK = 2.0 ** 90
EXPO = 0x7F800000
ORDER = ("sync", "gpsimd", "scalar", "tensor", "vector")


class Sem:

    def __init__(self, handle, k=1):
        self.h, self.k, self.n = handle, k, 0


class Slot:

    def __init__(self, t):
        self.t, self.free = t, []


class Ring:
    def __init__(self, slots):
        self.slots, self.i = slots, -1

    def next(self):
        self.i = (self.i + 1) % len(self.slots)
        return self.slots[self.i]


class Rec:
    pass


class Queues:

    def __init__(self):
        self.q = {e: [] for e in ORDER}

    def do(self, eng, fn, waits=(), inc=None):
        self.q[eng].append((list(waits), fn, inc))
        if inc is None:
            return None
        inc.n += inc.k
        return (inc, inc.n)

    def emit(self, name, eng):
        seen = {}
        for waits, fn, inc in self.q[name]:
            need = {}
            for s, v in waits:
                need[s] = max(need.get(s, 0), v)
            for s, v in need.items():
                if seen.get(s, 0) < v:
                    eng.wait_ge(s.h, v)
                    seen[s] = v
            ins = fn(eng)
            if inc is not None:
                ins.then_inc(inc.h, inc.k)


def macaron_kernel(nc, x_d, wk_d, wqk_d, gw_d, gain_d, bias_d, lg_d, out_d, hs_d, ys_d):
    with ExitStack() as ctx:
        def sb(name, shape, dt):
            return ctx.enter_context(nc.sbuf_tensor("t_" + name, shape, dt))

        def sem(name, k=1):
            return Sem(ctx.enter_context(nc.semaphore(name)), k)

        Q = Queues()
        do = Q.do

        def pe(fn, waits=(), inc=None):
            return do("tensor", fn, waits, inc)

        def dve(fn, waits=(), inc=None):
            return do("vector", fn, waits, inc)

        def act(fn, waits=(), inc=None):
            return do("scalar", fn, waits, inc)

        def pool(fn, waits=(), inc=None):
            return do("gpsimd", fn, waits, inc)

        def sp(fn, waits=(), inc=None):
            return do("sync", fn, waits, inc)

        W = sb("W", [128, 26, 1024], F32)
        W16 = W[:, :, :].rearrange("p a b -> p (a b)").bitcast(F16)
        X = sb("X", [128, NT, D], F32)
        identf = sb("identf", [128, 128], F32)
        ident16 = sb("ident16", [128, 128], F16)
        identb = sb("identb", [128, 128], BF16)
        ones16 = sb("ones16", [128, 128], F16)
        tri = sb("tri", [128, 128], F16)
        maskf = sb("maskf", [128, 128], F32)
        maskb = sb("maskb", [128, 128], BF16)
        row0 = sb("row0", [128, 128], F16)
        extra0 = sb("extra0", [128, 1], F32)
        mhalf = sb("mhalf", [128, 4], F32)
        zrow = sb("zrow", [128, 512], F16)
        ebi = sb("ebi", [128, 8], I32)
        ebase = sb("ebase", [128, 8], F32)
        ebpi = sb("ebpi", [128, 8], I32)
        ebp = sb("ebp", [128, 8], F32)
        tie = sb("tie", [128, 8], F32)
        tiei = sb("tiei", [128, 8], I32)
        jioi = sb("jioi", [128, 8], I32)
        jio = sb("jio", [128, 8], F32)
        gain = W[:, 24, 3 * D:4 * D]
        bias = sb("bias", [128, D], F32)
        gw = sb("gw", [128, 2, 8], F32)
        wqk = sb("wqk", [128, 2, 64], F32)
        wqh = sb("wqh", [128, 2, 64], F16)
        wql = sb("wql", [128, 2, 64], F16)
        WQ = sb("WQ", [128, 2, 2, 2, 96], F16)
        lg = sb("lg", [128, 2], F32)
        lt = sb("lt", [128, 8], F32)
        MX = sb("MX", [128, 25], F32)
        M3 = sb("M3", [128, 3], F32)
        MA = sb("MA", [128, 3], F32)
        MP = sb("MP", [128, 3], F32)
        SC = sb("SC", [128, 3], F32)
        K = sb("K", [128, 8], F32)
        HP = Ring([Slot(sb(f"hp{i}", [128, 4, D], F32)) for i in range(3)])
        S16 = Ring([Slot(sb(f"s16{i}", [128, 4, 512], F16)) for i in range(3)])
        BS = Ring([Slot(sb(f"bs{i}", [128, 4, 6], F32)) for i in range(3)])
        MV = Ring([Slot(sb(f"mv{i}", [128, 4, 2], F32)) for i in range(3)])
        VE = Ring([Slot(sb(f"ve{i}", [128, 2, 4], F32)) for i in range(3)])
        HT32 = Slot(sb("ht32", [128, 1024], F32))
        RT = Ring([Slot(sb(f"rt{i}", [128, 6, 4, 8], F32)) for i in range(3)])
        RS = Ring([Slot(sb(f"rs{i}", [128, 10, 4], F32)) for i in range(3)])
        M16 = Ring([Slot(sb(f"m16{i}", [128, 4, 8], F16)) for i in range(3)])
        CP = sb("CP", [128, NTC + 1, 8], F16)
        cp_free = []
        POS = sb("POS", [128, 2, 2, NT], I32)
        POSY = sb("POSY", [128, 2, 2, NT], I32)
        OH = sb("OH", [128, 2, NTC, 8], F16)
        OF = sb("OF", [128, 2, NTC, 8], F32)
        OS = sb("OS", [128, 2, NTC], F32)
        oh_free = []
        tok = {}
        DL = sb("DL", [128, 8], F32)
        CW = sb("CW", [128, 2, 2, NT], F32)
        TT = sb("TT", [128, 6, 8], F32)
        NTI = sb("NTI", [128, 8], I32)
        PADI = sb("PADI", [128, 8], I32)
        TJ = sb("TJ", [NJ, 2, 8], F32)
        TR = sb("TR", [NJ, 4], F32)
        TAB = [[sb(f"tab{l}{c}", [NJ, 2], I32) for c in range(C)] for l in range(2)]
        HTA = Slot(sb("hta", [128, 4, 512], F16))
        QS = Slot(sb("QS", [96, 512], F16))
        KS = Slot(sb("KS", [96, 512], F16))
        SIM = Ring([Slot(sb(f"sim{i}", [128, 512], F32)) for i in range(2)])
        PH = Ring([Slot(sb(f"ph{i}", [128, 2, 512], F16)) for i in range(2)])
        AT = Ring([Slot(sb(f"at{i}", [128, 16], F32)) for i in range(4)])
        SI = Ring([Slot(sb(f"si{i}", [128, 512], F16)) for i in range(4)])
        HT = Ring([Slot(sb(f"ht{i}", [128, 512], F16)) for i in range(2)])
        TH = Ring([Slot(sb(f"th{i}", [128, 512], F32)) for i in range(1)])
        GF = Ring([Slot(sb(f"gf{i}", [128, 512], F32)) for i in range(1)])
        GH = Ring([Slot(sb(f"gh{i}", [128, 2, 512], F16)) for i in range(2)])
        YO = Ring([Slot(W[:, 24, D * i:D * i + D]) for i in range(3)])
        YG = Ring([Slot(W[:, 25, 512 * i:512 * i + 512].rearrange("p (k d) -> p k d", k=2)) for i in range(2)])

        B = [Slot(ctx.enter_context(nc.psum_tensor(f"B{i}", [128, 512], F32))) for i in range(8)]

        d_x = [sem(f"d_x{i}", 16) for i in range(8)]
        d_w = [sem(f"d_w{i}", 16) for i in range(6)]
        d_c = [sem(f"d_c{i}", 16) for i in range(5)]
        d_in = [sem(f"d_in{i}", 16) for i in range(4)]
        d_y = [sem(f"d_y{i}", 16) for i in range(3)]
        d_sc = [sem(f"d_sc{i}", 16) for i in range(3)]
        d_pad = sem("d_pad", 16)
        d_z = sem("d_z", 16)
        d_g = [sem(f"d_g{i}", 16) for i in range(2)]
        d_o = sem("d_o", 16)
        s_k = sem("s_k")
        s_kd = sem("s_kd")
        s_ka = sem("s_ka")
        s_wh = sem("s_wh")
        s_wl = sem("s_wl")
        s_mx = sem("s_mx")
        s_ln = sem("s_ln")
        s_pw = sem("s_pw")
        s_hh = sem("s_hh")
        s_tp = sem("s_tp")
        s_tc = sem("s_tc")
        s_gs = sem("s_gs")
        s_rt = sem("s_rt")
        s_e2 = sem("s_e2")
        s_rk = sem("s_rk")
        s_tab = sem("s_tab")
        s_tin = sem("s_tin")
        s_ht = sem("s_ht")
        s_x1 = sem("s_x1")
        s_x3 = sem("s_x3")
        s_th = sem("s_th")
        s_g = sem("s_g")
        s_gt = sem("s_gt")
        s_gh = sem("s_gh")
        s_gl = sem("s_gl")
        s_y = sem("s_y")
        s_yc = sem("s_yc")
        s_x = sem("s_x")
        s_at = sem("s_at")
        s_ac = sem("s_ac")
        s_sim = sem("s_sim")
        s_sco = sem("s_sco")
        s_top = sem("s_top")
        s_p = sem("s_p")
        s_pt = sem("s_pt")
        s_ps = sem("s_ps")
        s_msg = sem("s_msg")
        s_bl = sem("s_bl")
        s_pb = sem("s_pb")
        s_gelu = sem("s_gelu")

        block = ctx.enter_context(nc.Block())

        k1 = pool(lambda e: e.memset(identf[:], 0.0), inc=s_k)
        k2 = pool(lambda e: e.memset(ones16[:], 1.0), inc=s_k)
        k3 = pool(lambda e: e.memset(maskf[:], 0.0), inc=s_k)
        pool(lambda e: e.memset(row0[:], 0.0), inc=s_k)
        pool(lambda e: e.memset(extra0[:], 0.0), inc=s_k)
        pool(lambda e: e.memset(mhalf[:], -0.5), inc=s_k)
        k_half = (s_k, s_k.n)
        pool(lambda e: e.memset(zrow[:], 0.0), inc=s_k)
        pool(lambda e: e.iota(ebi[:], pattern=[[CAP, 8]], base=0, channel_multiplier=0), inc=s_k)
        pool(lambda e: e.iota(ebpi[:], pattern=[[CAP, 8]], base=0, channel_multiplier=1), inc=s_k)
        pool(lambda e: e.iota(tiei[:], pattern=[[-1, 8]], base=8, channel_multiplier=0), inc=s_k)
        pool(lambda e: e.iota(jioi[:], pattern=[[0, 8]], base=0, channel_multiplier=1), inc=s_k)
        kz = (s_k, s_k.n)
        pool(lambda e: e.affine_select(out=identf[:], in_=identf[:], compare_op=ALU.not_equal, fill=1.0, base=0,
                                       pattern=[[-1, 128]], channel_multiplier=1), [kz], s_k)
        pool(lambda e: e.affine_select(out=tri[:], in_=ones16[:], compare_op=ALU.is_gt, fill=0.0, base=0,
                                       pattern=[[1, 128]], channel_multiplier=-1), [kz], s_k)
        pool(lambda e: e.affine_select(out=maskf[:], in_=maskf[:], compare_op=ALU.is_gt, fill=NEG, base=0,
                                       pattern=[[-1, 128]], channel_multiplier=1), [kz], s_k)
        pool(lambda e: e.affine_select(out=extra0[:], in_=extra0[:], compare_op=ALU.not_equal, fill=384.0, base=0,
                                       pattern=[[0, 1]], channel_multiplier=1), [kz], s_k)
        pool(lambda e: e.memset(row0[:, 0:1], 2.0 ** 14), [kz], s_k)
        kc = (s_k, s_k.n)
        for a, b in ((ident16, identf), (identb, identf), (maskb, maskf), (ebase, ebi), (ebp, ebpi),
                     (tie, tiei), (jio, jioi)):
            dve(lambda e, a=a, b=b: e.tensor_copy(a[:], b[:]), [kc], s_kd)
        kd = (s_kd, s_kd.n)

        xv = x_d.rearrange("(n p) d -> p n d", p=128)
        ov = out_d.rearrange("(n p) d -> p n d", p=128)
        x_ready = []
        for i in range(8):
            x_ready.append(sp(lambda e, i=i: e.dma_start(X[:, 4 * i:4 * i + 4, :], xv[:, 4 * i:4 * i + 4, :]),
                              inc=d_x[i]))
            if i == 0:
                ld_gw = sp(lambda e: e.dma_start(gw[:], gw_d), inc=d_c[0])
                ld_qk = sp(lambda e: e.dma_start(wqk[:], wqk_d), inc=d_c[1])
                ld_lg = sp(lambda e: e.dma_start(lg[:], lg_d), inc=d_c[2])
        x_ready = [x_ready[i // 4] for i in range(NT)]
        w_ready = []
        for i in range(6):
            w_ready.append(sp(lambda e, i=i: e.dma_start(W[:, 4 * i + 2:4 * i + 6, :], wk_d[:, 4 * i:4 * i + 4, :]),
                              inc=d_w[i]))
        ld_bi = sp(lambda e: e.dma_start(bias[:], bias_d), inc=d_c[4])
        z_rows = []
        for l in range(2):
            for c in range(C):
                z_rows.append(sp(lambda e, l=l, c=c: e.dma_start(hs_d[l][c][SPARE:SPARE + 128, :], zrow[:]),
                                 [kz], d_z))

        def maxima():
            for k in range(24):
                t = dve(lambda e, k=k: e.tensor_reduce(MX[:, k:k + 1], W[:, k + 2, :], AX.X, ALU.max,
                                                       apply_absolute_value=True), [w_ready[k // 4]], s_mx)
                yield
            t = dve(lambda e: e.tensor_reduce(MX[:, 24:25], wqk[:].rearrange("p a b -> p (a b)"), AX.X, ALU.max,
                                              apply_absolute_value=True), [ld_qk], s_mx)
            dve(lambda e: e.tensor_reduce(M3[:, 0:1], MX[:, 0:16], AX.X, ALU.max), [t], s_mx)
            dve(lambda e: e.tensor_reduce(M3[:, 1:2], MX[:, 16:24], AX.X, ALU.max), [t], s_mx)
            a = dve(lambda e: e.tensor_copy(M3[:, 2:3], MX[:, 24:25]), [t], s_mx)
            b = pool(lambda e: e.partition_all_reduce(MA[:], M3[:], 128, bass.bass_isa.ReduceOp.max), [a], s_pw)
            b = dve(lambda e: e.tensor_scalar(MA[:], MA[:], 2.0 ** -30, None, ALU.max), [b], s_mx)
            b = dve(lambda e: e.tensor_scalar(MP[:].bitcast(I32), MA[:].bitcast(I32), EXPO, None, ALU.bitwise_and),
                    [b], s_mx)
            b = dve(lambda e: e.tensor_scalar(SC[:].bitcast(I32), MP[:].bitcast(I32), -1.0, float(268 << 23),
                                              ALU.mult, ALU.add), [b], s_mx)
            dve(lambda e: e.tensor_scalar(K[:, 0:1], MP[:, 0:1], 2.0 ** -25, None, ALU.mult), [b], s_mx)
            dve(lambda e: e.tensor_scalar(K[:, 1:2], MP[:, 0:1], MP[:, 0:1], MP[:, 1:2], ALU.mult, ALU.mult), [b], s_mx)
            a = dve(lambda e: e.tensor_scalar(K[:, 2:3], MP[:, 2:3], MP[:, 2:3], 2.0 ** -12 / 32 ** 0.5,
                                              ALU.mult, ALU.mult), [b], s_mx)
            dve(lambda e: e.tensor_scalar(K[:, 1:2], K[:, 1:2], 2.0 ** -12, None, ALU.mult), [a], s_mx)
            tok["kk"] = dve(lambda e: e.tensor_scalar(K[:, 3:4], K[:, 2:3], -1.0, None, ALU.mult), [a], s_mx)

        def split():
            scaled = tok["kk"]
            l = [None] * 24
            h = [None] * 24
            for k in range(24):
                o = k * 2048
                s = SC[:, 0:1] if k < 16 else SC[:, 1:2]
                w = [scaled]
                if k >= 2:
                    w.append(l[k - 2])
                h[k] = act(lambda e, k=k, o=o, s=s: e.activation(W16[:, o:o + 1024], W[:, k + 2, :], ACT.Copy,
                                                                 scale=s), w, s_wh)
                l[k] = dve(lambda e, k=k, o=o, s=s: e.scalar_tensor_tensor(
                    out=W16[:, o + 1024:o + 2048], in0=W[:, k + 2, :], scalar=s, in1=W16[:, o:o + 1024],
                    op0=ALU.mult, op1=ALU.subtract), [h[k]], s_wl)
            tok["w"] = l[23]
            tok["gain"] = sp(lambda e: e.dma_start(gain, gain_d), [l[23]], d_c[3])
            for slot in YO.slots + YG.slots:
                slot.free = [l[23]]

        def split_qk():
            a = dve(lambda e: e.tensor_scalar(wqh[:], wqk[:], SC[:, 2:3], None, ALU.mult), [tok["kk"]], s_wl)
            a = dve(lambda e: e.scalar_tensor_tensor(out=wql[:], in0=wqk[:], scalar=SC[:, 2:3], in1=wqh[:],
                                                     op0=ALU.mult, op1=ALU.subtract), [a], s_wl)
            for r in range(3):
                for m in range(2):
                    dve(lambda e, r=r, m=m: e.tensor_copy(WQ[:, :, 0, m, 32 * r:32 * r + 32],
                                                          wqh[:, :, 32 * m:32 * m + 32]), [a], s_wl)
                    w = dve(lambda e, r=r, m=m: e.tensor_copy(WQ[:, :, 1, m, 32 * r:32 * r + 32],
                                                              wql[:, :, 32 * m:32 * m + 32]), [a], s_wl)
            tok["wq"] = w

        def scalars():
            a = act(lambda e: e.activation(lt[:, 0:1], lg[:, 0:1], ACT.Tanh, scale=0.5), [ld_lg], s_ka)
            b = dve(lambda e: e.tensor_scalar(lt[:, 1:2], lg[:, 1:2], -1.0, None, ALU.mult), [ld_lg], s_kd)
            b = dve(lambda e: e.tensor_tensor(lt[:, 2:3], lt[:, 1:2], lg[:, 1:2], ALU.min), [b], s_kd)
            b = act(lambda e: e.activation(lt[:, 3:4], lt[:, 2:3], ACT.Exp), [b], s_ka)
            b = dve(lambda e: e.tensor_scalar(lt[:, 4:5], lt[:, 3:4], 1.0, None, ALU.add), [b], s_kd)
            b = act(lambda e: e.activation(lt[:, 5:6], lt[:, 4:5], ACT.Ln), [b], s_ka)
            c = dve(lambda e: e.tensor_scalar(lt[:, 6:7], lg[:, 1:2], 0.0, 0.01, ALU.max, ALU.add), [b], s_kd)
            dve(lambda e: e.tensor_tensor(K[:, 6:7], lt[:, 5:6], lt[:, 6:7], ALU.add), [c], s_kd)
            dve(lambda e: e.tensor_scalar(K[:, 4:5], lt[:, 0:1], 0.5, 0.5, ALU.mult, ALU.add), [a], s_kd)
            return dve(lambda e: e.tensor_scalar(K[:, 5:6], lt[:, 0:1], -0.5, 0.5, ALU.mult, ALU.add), [a], s_kd)

        def norm(t0, r):
            hp, s16, bs, mv, ve = HP.next(), S16.next(), BS.next(), MV.next(), VE.next()
            r.hp, r.s16, r.sc_sem = hp, s16, d_sc[S16.i]
            for j in range(4):
                a = dve(lambda e, j=j: e.bn_stats(bs.t[:, j, :], X[:, t0 + j, :]), [x_ready[t0 + j]] + bs.free, s_ln)
                bs.free = []
                if j == 1:
                    yield
            st = a
            for j in range(4):
                a = dve(lambda e, j=j: e.bn_aggr(mv.t[:, j, :], bs.t[:, j, :]), [st] + mv.free, s_ln)
                mv.free = []
            a = dve(lambda e: e.tensor_scalar(ve.t[:, 0, :], mv.t[:, :, 1], 1e-5, 2.0 ** -20, ALU.add, ALU.mult),
                    [a] + ve.free, s_ln)
            p = pool(lambda e: e.tensor_tensor(ve.t[:, 1, :], ve.t[:, 0, :], mhalf[:], ALU.pow), [a, k_half], s_pw)
            yield
            r.hp_t, hh_t, r.hl_t = [], [], []
            for j in range(4):
                r.hp_t.append(dve(lambda e, j=j: e.tensor_scalar(
                    hp.t[:, j, :], X[:, t0 + j, :], mv.t[:, j, 0:1], ve.t[:, 1, j:j + 1],
                    ALU.subtract, ALU.mult), [p] + hp.free, s_ln))
                hh_t.append(act(lambda e, j=j: e.activation(s16.t[:, j, 0:256], hp.t[:, j, :], ACT.Copy),
                                [r.hp_t[j]] + s16.free, s_hh))
            yield
            for j in range(4):
                r.hl_t.append(dve(lambda e, j=j: e.tensor_tensor(s16.t[:, j, 256:512], hp.t[:, j, :],
                                                                 s16.t[:, j, 0:256], ALU.subtract),
                                  [hh_t[j]], s_ln))
                if j == 1:
                    yield
            hp.free, s16.free = [], []
            bs.free, mv.free, ve.free = [r.hl_t[-1]], [r.hl_t[-1]], [r.hl_t[-1]]

        def router(L, c, g, bank, turn):
            r = Rec()
            t0 = c * NTC + 4 * g
            yield from norm(t0, r)
            hp, s16 = r.hp, r.s16
            yield
            for h in range(2):
                for j in (2 * h, 2 * h + 1):
                    for b in range(2):
                        o = 256 * (j % 2) + 128 * b
                        tp = pe(lambda e, j=j, b=b, o=o: e.transpose(
                            bank.t[:, o:o + 128], hp.t[:, j, 128 * b:128 * b + 128], identf[:]),
                            [r.hp_t[j], kd] + bank.free, s_tp)
                tc = act(lambda e, h=h: e.activation(HT32.t[:, 512 * h:512 * h + 512], bank.t[:], ACT.Copy),
                         [tp] + HT32.free, s_tc)
                bank.free = [tc]
                yield
            HT32.free = []
            for j in range(4):
                for b in range(2):
                    gs = pe(lambda e, j=j, b=b: e.matmul(
                        bank.t[:, 8 * j:8 * j + 8], HT32.t[:, 256 * j + 128 * b:256 * j + 128 * b + 128], gw[:, b, :],
                        start=b == 0, stop=b == 1), [tc, ld_gw] + bank.free, s_gs)
            HT32.free = [gs]
            hp.free = [tp, r.hl_t[-1]]
            while turn["route"] != (L, c, g):
                yield
            rt = RT.next()
            rs, m16 = RS.next(), M16.next()
            R, S = rt.t, rs.t
            sc = dve(lambda e: e.tensor_copy(R[:, 0], bank.t[:, 0:32].rearrange("p (a b) -> p a b", a=4)),
                     [gs] + rt.free, s_rt)
            bank.free = [sc]
            yield

            def bc(ap):
                return ap.unsqueeze(2).to_broadcast([128, 4, 8])

            tieb = tie[:].unsqueeze(1).to_broadcast([128, 4, 8])
            chain = [sc] + rs.free + m16.free

            def step(fn):
                t = dve(fn, list(chain), s_rt)
                chain[:] = [t]
                return t

            for k, (src, oh) in enumerate(((0, 2), (3, 4))):
                step(lambda e, src=src, k=k: e.tensor_reduce(S[:, k], R[:, src], AX.X, ALU.max))
                step(lambda e, src=src, k=k: e.tensor_tensor(R[:, 1], R[:, src], bc(S[:, k]), ALU.is_equal))
                step(lambda e: e.tensor_tensor(R[:, 1], R[:, 1], tieb, ALU.mult))
                step(lambda e: e.tensor_reduce(S[:, 2], R[:, 1], AX.X, ALU.max))
                step(lambda e, oh=oh: e.tensor_tensor(R[:, oh], R[:, 1], bc(S[:, 2]), ALU.is_equal))
                if k == 0:
                    step(lambda e: e.scalar_tensor_tensor(out=R[:, 3], in0=R[:, 2], scalar=-3e38, in1=R[:, 0],
                                                          op0=ALU.mult, op1=ALU.add))
                    yield
            df = step(lambda e: e.tensor_tensor(S[:, 3], S[:, 1], S[:, 0], ALU.subtract))
            ex = act(lambda e: e.activation(S[:, 4], S[:, 3], ACT.Exp, scale=2.0 ** -10), [df], s_e2)
            mm = step(lambda e: e.tensor_tensor(m16.t[:], R[:, 2], R[:, 4], ALU.add))
            if g == 0:
                step(lambda e: e.memset(CP[:, 0, :], 0.0))
            for j in range(4):
                cp = step(lambda e, j=j: e.tensor_tensor(CP[:, 4 * g + j + 1, :], CP[:, 4 * g + j, :], m16.t[:, j, :],
                                                         ALU.add))
            pe(lambda e: e.matmul(bank.t[:, 0:32], tri[:], m16.t[:].rearrange("p a b -> p (a b)"),
                                  start=True, stop=False), [mm, kd] + bank.free)
            rk = pe(lambda e: e.matmul(bank.t[:, 0:32], ones16[:], CP[:, 4 * g:4 * g + 4, :].rearrange(
                "p a b -> p (a b)"), start=False, stop=True), [cp], s_rk)
            chain.extend(oh_free)
            for k, oh in enumerate((2, 4)):
                step(lambda e, oh=oh, k=k: e.tensor_copy(OH[:, k, 4 * g:4 * g + 4, :], R[:, oh]))
            yield
            chain.append(rk)
            rb = step(lambda e: e.tensor_tensor(R[:, 5], bank.t[:, 0:32].rearrange("p (a b) -> p a b", a=4),
                                                ebase[:].unsqueeze(1).to_broadcast([128, 4, 8]), ALU.add))
            bank.free = [rb]
            for k, oh in enumerate((2, 4)):
                step(lambda e, oh=oh: e.tensor_tensor(R[:, oh], R[:, oh], R[:, 5], ALU.mult))

                def total(e, oh=oh, k=k):
                    with nc.allow_low_precision(reason="whole numbers"):
                        return e.tensor_reduce(POS[:, L, k, t0:t0 + 4], R[:, oh], AX.X, ALU.add)
                ps = step(total)
            for j in range(4):
                for k in range(2):
                    sd = pool(lambda e, j=j, k=k: e.indirect_dma_start(
                        hs_d[L][c], bass.IndirectOffsetOnAxis(ap=POS[:, L, k, t0 + j:t0 + j + 1], axis=0),
                        s16.t[:, j, :], None), [ps, r.hl_t[j]], r.sc_sem)
            s16.free = [sd]
            tok["scattered", L, c, g] = sd
            yield
            chain.append(ex)
            step(lambda e: e.tensor_scalar(S[:, 5], S[:, 4], 1.0, None, ALU.add))
            step(lambda e: e.reciprocal(S[:, 6], S[:, 5]))
            cw = step(lambda e: e.tensor_tensor(S[:, 7], S[:, 6], S[:, 4], ALU.mult))
            step(lambda e: e.tensor_copy(CW[:, L, 0, t0:t0 + 4], S[:, 6]))
            cw = step(lambda e: e.tensor_copy(CW[:, L, 1, t0:t0 + 4], S[:, 7]))
            rt.free, rs.free, m16.free = [cw], [cw], [rk, cw]
            turn["route"] = (L, c, g + 1)
            tok["cp"] = cp

        def tables(L, c, bank):
            cn = pe(lambda e: e.matmul(bank.t[:, 0:8], ones16[:], CP[:, NTC, :], start=True, stop=True),
                    [tok["cp"]] + bank.free, s_rk)
            chain = [cn] + tab_free
            yield

            def step(fn):
                t = dve(fn, list(chain), s_tab)
                chain[:] = [t]
                return t

            ne = step(lambda e: e.tensor_copy(TT[:, 0], bank.t[:, 0:8]))
            bank.free = [ne]
            pi = step(lambda e: e.tensor_tensor(PADI[:], TT[:, 0], ebp[:], ALU.add))
            for i in range(8):
                pd = pool(lambda e, i=i: e.indirect_dma_start(
                    hs_d[L][c], bass.IndirectOffsetOnAxis(ap=PADI[:, i:i + 1], axis=0), zrow[:], None), [pi, kc], d_pad)
            step(lambda e: e.tensor_scalar(NTI[:], TT[:, 0], 127.0, None, ALU.add))
            step(lambda e: e.tensor_scalar(NTI[:], NTI[:], 7, None, ALU.arith_shift_right))
            step(lambda e: e.tensor_copy(TT[:, 1], NTI[:]))
            step(lambda e: e.memset(TT[:, 3], 0.0))
            step(lambda e: e.tensor_tensor_scan(TT[:, 2], TT[:, 1], TT[:, 3], 0.0, ALU.add, ALU.add))
            step(lambda e: e.tensor_tensor(TJ[:, 0], TT[0:NJ, 2], jio[0:NJ], ALU.is_le))
            step(lambda e: e.tensor_tensor(TJ[:, 1], TJ[:, 0], TT[0:NJ, 1], ALU.mult))
            step(lambda e: e.tensor_reduce(TR[:, 0:1], TJ[:, 0], AX.X, ALU.add))
            step(lambda e: e.tensor_reduce(TR[:, 1:2], TJ[:, 1], AX.X, ALU.add))
            step(lambda e: e.tensor_tensor(TR[:, 2:3], jio[0:NJ, 0:1], TR[:, 1:2], ALU.subtract))
            step(lambda e: e.tensor_scalar(TR[:, 2:3], TR[:, 2:3], 128.0, None, ALU.mult))
            step(lambda e: e.scalar_tensor_tensor(out=TR[:, 3:4], in0=TR[:, 0:1], scalar=float(CAP), in1=TR[:, 2:3],
                                                  op0=ALU.mult, op1=ALU.add))
            tab = TAB[L][c]
            step(lambda e: e.tensor_scalar(tab[:, 0:1], TR[:, 0:1], 7.0, None, ALU.min))
            t = step(lambda e: e.tensor_scalar(tab[:, 1:2], TR[:, 3:4], float(SPARE), None, ALU.min))
            tok["table", L, c] = t
            tok["ready", L, c] = [tok["scattered", L, c, g] for g in range(NG)] + [pd, z_rows[-1]]
            yield
            step(lambda e: e.tensor_tensor(DL[:], TT[:, 2], TT[:, 1], ALU.subtract))
            step(lambda e: e.scalar_tensor_tensor(out=DL[:], in0=DL[:], scalar=128.0, in1=ebase[:],
                                                  op0=ALU.mult, op1=ALU.subtract))
            for k in range(2):
                step(lambda e, k=k: e.tensor_tensor(OF[:, k], OH[:, k], DL[:].unsqueeze(1).to_broadcast(
                    [128, NTC, 8]), ALU.mult))
                step(lambda e, k=k: e.tensor_reduce(OS[:, k], OF[:, k], AX.X, ALU.add))
                yp = step(lambda e, k=k: e.tensor_tensor(
                    POSY[:, L, k, c * NTC:c * NTC + NTC], OS[:, k], POS[:, L, k, c * NTC:c * NTC + NTC], ALU.add))
            oh_free[:] = [yp]
            chain.append(tok["kk"])
            t = step(lambda e: e.tensor_scalar(CW[:, L, :, c * NTC:c * NTC + NTC], CW[:, L, :, c * NTC:c * NTC + NTC],
                                               K[:, 1:2], None, ALU.mult))
            tok["ypos", L, c] = t
            tab_free[:] = [t, pd]

        def experts(side):
            seq = [(L, c, j) for L in range(2) for c in range(C) for j in range(NJ)]
            ein, htt, gt, turned, out = {}, {}, {}, {}, {}

            def load(n):
                L, c, j = seq[n]
                tab = TAB[L][c]
                while ("table", L, c) not in tok:
                    side.step()
                s = SI.next()

                def f(e):
                    r = e.value_load(tab[j:j + 1, 1:2], min_val=0, max_val=SPARE)
                    return e.dma_start(s.t[:], hs_d[L][c][bass.ds(r, 128), :])
                t = sp(f, [tok["table", L, c]] + tok["ready", L, c] + s.free, d_in[SI.i])
                s.free = []
                ein[n] = (s, t)

            def tin(n):
                s, t = ein.pop(n)
                b = B[3]
                b16 = b.t[:].bitcast(F16)
                for k in range(4):
                    a = pe(lambda e, k=k: e.transpose(b16[:, 128 * k:128 * k + 128], s.t[:, 128 * k:128 * k + 128],
                                                      ident16[:]), [t, kd] + b.free, s_tin if k == 3 else None)
                s.free = [a]
                h = HT.next()
                h_t = dve(lambda e: e.tensor_copy(h.t[:], b16[:, 0:512]), [a] + h.free, s_ht)
                b.free = [h_t]
                htt[n] = (h, h_t)

            def ups(n, w, hold):
                L, c, j = seq[n]
                tab = TAB[L][c]
                h, h_t = htt[n]
                bank, s = (B[1], s_x1) if w == 0 else (B[2], s_x3)
                k = 0
                for db in range(2):
                    for hl, wl in ((0, 0), (0, 1), (1, 0)):
                        def f(e, db=db, hl=hl, wl=wl, k=k):
                            if w == 0 and k == 0:
                                hold["r"] = e.value_load(tab[j:j + 1, 0:1], min_val=0, max_val=7)
                            return e.matmul(bank.t[:], h.t[:, (2 * hl + db) * 128:(2 * hl + db) * 128 + 128],
                                            W16[:, bass.ds(hold["r"] * 4096 + (db * 2048 + wl * 1024 + w * 512), 512)],
                                            start=k == 0, stop=k == 5)
                        a = pe(f, [h_t, tok["w"], tok["table", L, c]] + bank.free, s if k == 5 else None)
                        k += 1
                return a

            def up_a(n, hold):
                x1 = ups(n, 0, hold)
                th = TH.next()
                a = act(lambda e: e.activation(th.t[:], B[1].t[:], ACT.Tanh, scale=K[:, 0:1]),
                        [x1, tok["kk"]] + th.free, s_th)
                hold["a"] = a
                hold["th"] = th

            def up_b(n, hold):
                hold["x3"] = ups(n, 1, hold)
                htt.pop(n)[0].free = [hold["x3"]]

            def gate(n, hold):
                x3, a, th = hold["x3"], hold["a"], hold["th"]
                b = dve(lambda e: e.scalar_tensor_tensor(out=th.t[:], in0=th.t[:], scalar=1.0, in1=B[1].t[:],
                                                         op0=ALU.add, op1=ALU.mult), [a], s_g)
                B[1].free = [b]
                g = GF.next()
                b = dve(lambda e: e.scalar_tensor_tensor(out=g.t[:], in0=B[2].t[:], scalar=2.0 ** -52, in1=th.t[:],
                                                         op0=ALU.mult, op1=ALU.mult), [b, x3] + g.free, s_g)
                B[2].free = [b]
                th.free = [b]
                gt[n] = (g, b)

            def turn(n):
                g, g_t = gt.pop(n)
                b = B[3]
                for k in range(4):
                    a = pe(lambda e, k=k: e.transpose(b.t[:, 128 * k:128 * k + 128], g.t[:, 128 * k:128 * k + 128],
                                                      identf[:]), [g_t] + b.free, s_gt if k == 3 else None)
                g.free = [a]
                turned[n] = a

            def parts(n):
                a, b = turned.pop(n), B[3]
                gh = GH.next()
                a = act(lambda e: e.activation(gh.t[:, 0, :], b.t[:], ACT.Copy), [a] + gh.free, s_gh)
                a = dve(lambda e: e.tensor_tensor(gh.t[:, 1, :], b.t[:], gh.t[:, 0, :], ALU.subtract), [a], s_gl)
                b.free = [a]
                out[n] = (gh, a)

            def down(n):
                L, c, j = seq[n]
                tab = TAB[L][c]
                gh, a = out.pop(n)
                b = B[4]
                hold = {}
                k = 0
                for fb in range(4):
                    for gl, wl in ((0, 0), (0, 1), (1, 0)):
                        def f(e, fb=fb, gl=gl, wl=wl, k=k):
                            if k == 0:
                                hold["r"] = e.value_load(tab[j:j + 1, 0:1], min_val=0, max_val=7)
                            return e.matmul(b.t[:, 0:256], gh.t[:, gl, fb * 128:fb * 128 + 128],
                                            W16[:, bass.ds(hold["r"] * 2048 + (W2OFF + wl * 1024 + fb * 256), 256)],
                                            start=k == 0, stop=k == 11)
                        t = pe(f, [a] + b.free, s_y if k == 11 else None)
                        k += 1
                gh.free = [t]
                yo = YO.next()
                yc = act(lambda e: e.activation(yo.t, b.t[:, 0:256], ACT.Copy), [t] + yo.free, s_yc)
                b.free = [yc]
                t = sp(lambda e: e.dma_start(ys_d[L][c][128 * j:128 * j + 128, :], yo.t), [yc], d_y[YO.i])
                yo.free = [t]
                if j == NJ - 1:
                    tok["done", L, c] = [(s, s.n) for s in d_y]

            N = len(seq)
            for n in range(3):
                load(n)
            tin(0)
            for n in range(N + 2):
                if n + 3 < N:
                    load(n + 3)
                hold = {}
                if n < N:
                    up_a(n, hold)
                if n + 1 < N:
                    tin(n + 1)
                side.step()
                if n < N:
                    up_b(n, hold)
                if 1 <= n < N + 1:
                    turn(n - 1)
                if n < N:
                    gate(n, hold)
                if 1 <= n < N + 1:
                    parts(n - 1)
                side.step()
                if n >= 2:
                    down(n - 2)
                side.step()

        def combine(L, c, t0):
            for i in range(5):
                if i < 4:
                    yg = YG.next()
                    tile = t0 + i
                    for k in range(2):
                        t = pool(lambda e, k=k, yg=yg, tile=tile: e.indirect_dma_start(
                            yg.t[:, k, :], None, ys_d[L][c],
                            bass.IndirectOffsetOnAxis(ap=POSY[:, L, k, tile:tile + 1], axis=0)),
                            tok["done", L, c] + [tok["ypos", L, c]] + yg.free, d_g[YG.i])
                    nxt = (yg, tile, t)
                if i > 0:
                    yg, tile, t = old
                    a = t
                    for k in range(2):
                        a = dve(lambda e, k=k, yg=yg, tile=tile: e.scalar_tensor_tensor(
                            out=X[:, tile, :], in0=yg.t[:, k, :], scalar=CW[:, L, k, tile:tile + 1],
                            in1=X[:, tile, :], op0=ALU.mult, op1=ALU.add), [t, a], s_x)
                    yg.free = [a]
                    x_ready[tile] = a
                old = nxt
                yield

        def attend(b, r, tr, md):
            hp, s16, hl_t, hta = r.hp, r.s16, r.hl_t, HTA
            k_s, k_all = tok["ks"], tok["kk"]
            t16 = tr.t[:].bitcast(F16)
            H = hta.t
            for j in range(4):
                for k in range(4):
                    a = pe(lambda e, j=j, k=k: e.transpose(
                        t16[:, 128 * k:128 * k + 128], s16.t[:, j, 128 * k:128 * k + 128], ident16[:]),
                        [hl_t[j], kd] + tr.free, s_at if k == 3 else None)
                at_t = act(lambda e, j=j: e.activation(
                    H[:, :, 128 * j:128 * j + 128], t16[:, 0:512].rearrange("p (a b) -> p a b", a=4),
                    ACT.Copy), [a] + hta.free, s_ac)
                tr.free = [at_t]
                yield
            hta.free = []
            for m, dst in ((0, QS), (1, KS)):
                n = 0
                for db in range(2):
                    for wl, hl in ((0, 0), (0, 1), (1, 0)):
                        a = pe(lambda e, db=db, wl=wl, hl=hl, n=n, m=m: e.matmul(
                            tr.t[0:96, :], WQ[:, db, wl, m, :], H[:, 2 * hl + db, :], start=n == 0, stop=n == 5),
                            [at_t, tok["wq"]] + tr.free, s_at if n == 5 else None)
                        n += 1
                a = act(lambda e, dst=dst: e.activation(dst.t[:], tr.t[0:96, :], ACT.Copy, scale=2.0 ** -18),
                        [a] + dst.free, s_ac)
                yield
                lo = slice(64, 96) if m == 0 else slice(32, 64)
                a = dve(lambda e, dst=dst, lo=lo: e.scalar_tensor_tensor(
                    out=dst.t[lo, :], in0=tr.t[lo, :], scalar=2.0 ** -18, in1=dst.t[lo, :],
                    op0=ALU.mult, op1=ALU.subtract), [a], s_top)
                tr.free = [a]
                dst.free = []
                qk_t = a

            def row(i):
                n = 128 * (i + 1)
                bs, bq = B[5], B[6]
                k = 0
                for db in range(2):
                    for l, rr in ((0, 0), (0, 1), (1, 0)):
                        pe(lambda e, db=db, l=l, rr=rr, k=k: e.matmul(
                            bs.t[:, 0:n], H[:, 2 * l + db, 128 * i:128 * i + 128], H[:, 2 * rr + db, 0:n],
                            start=k == 0, stop=False), [at_t] + bs.free)
                        k += 1
                a = pe(lambda e: e.matmul(bs.t[:, n - 128:n], identb[:], maskb[:], start=False, stop=True), [kd], s_sim)
                q = pe(lambda e: e.matmul(bq.t[:, 0:n], QS.t[:, 128 * i:128 * i + 128], KS.t[:, 0:n],
                                          start=True, stop=True), [qk_t] + bq.free, s_sco)
                if i == 3:
                    QS.free, KS.free, hta.free = [q], [q], [q]
                yield
                sm, at = SIM.next(), AT.next()
                m = dve(lambda e: e.max(at.t[:, 0:8], bs.t[:, 0:n]), [a] + at.free, s_top)
                m = dve(lambda e: e.match_replace(sm.t[:, 0:n], at.t[:, 0:8], bs.t[:, 0:n], MARK),
                        [m] + sm.free, s_top)
                bs.free = [m]
                yield
                m = dve(lambda e: e.tensor_scalar(sm.t[:, 0:n], sm.t[:, 0:n], MARK, NEG, ALU.not_equal, ALU.mult),
                        [m], s_top)
                if i == 0:
                    m = dve(lambda e: e.tensor_tensor(sm.t[:, 0:128], sm.t[:, 0:128], maskf[:], ALU.min), [m], s_top)
                m = dve(lambda e: e.tensor_tensor_reduce(sm.t[:, 0:n], bq.t[:, 0:n], sm.t[:, 0:n], 1.0, -3e38,
                                                         ALU.add, ALU.max, at.t[:, 8:9]), [m, q], s_top)
                bq.free = [m]
                m = dve(lambda e: e.tensor_scalar(at.t[:, 9:10], at.t[:, 8:9], K[:, 3:4], None, ALU.mult),
                        [m, k_all], s_top)
                p = act(lambda e: e.activation(sm.t[:, 0:n], sm.t[:, 0:n], ACT.Exp, bias=at.t[:, 9:10],
                                               scale=K[:, 2:3], accum_out=at.t[:, 10:11]), [m], s_p)
                hm = act(lambda e: e.activation(hp.t[:, i, :], hp.t[:, i, :], ACT.Copy, scale=k_mix[:, 0:1]),
                         [hl_t[-1], k_s], s_ac)
                yield
                for s in range(i + 1):
                    a = pe(lambda e, s=s: e.transpose(tr.t[:, 128 * s:128 * s + 128],
                                                      sm.t[:, 128 * s:128 * s + 128], identf[:]),
                           [p] + tr.free, s_pt if s == i else None)
                sm.free = [a]
                rr = p
                if i == 0:
                    rr = dve(lambda e: e.tensor_tensor(at.t[:, 10:11], at.t[:, 10:11], extra0[:], ALU.add), [rr], s_top)
                rr = dve(lambda e: e.reciprocal(at.t[:, 11:12], at.t[:, 10:11]), [rr], s_top)
                rr = dve(lambda e: e.tensor_scalar(at.t[:, 12:13], at.t[:, 11:12], 0.0, 2.0 ** -24,
                                                   ALU.max, ALU.mult), [rr], s_top)
                rr = dve(lambda e: e.tensor_scalar(at.t[:, 13:14], at.t[:, 12:13], K[:, 5:6], None, ALU.mult),
                         [rr, k_s], s_top)
                ph, ms = PH.next(), md
                a = dve(lambda e: e.tensor_scalar(ph.t[:, 0, 0:n], tr.t[:, 0:n], 0.0, 2.0 ** 14, ALU.max, ALU.mult),
                        [a] + ph.free, s_ps)
                a = dve(lambda e: e.scalar_tensor_tensor(
                    out=ph.t[:, 1, 0:n], in0=tr.t[:, 0:n], scalar=2.0 ** 14, in1=ph.t[:, 0, 0:n],
                    op0=ALU.mult, op1=ALU.subtract), [a], s_ps)
                tr.free = [a]
                yield
                terms = [(ph.t[:, l, 128 * s:128 * s + 128], s, r2) for s in range(i + 1)
                         for l, r2 in ((0, 0), (0, 1), (1, 0))]
                if i == 0:
                    terms += [(row0[:], s, r2) for s in range(1, 4) for r2 in range(2)]
                for z, (lhs, s, r2) in enumerate(terms):
                    last = z == len(terms) - 1
                    g = pe(lambda e, lhs=lhs, s=s, r2=r2, z=z, last=last: e.matmul(
                        ms.t[:, 0:256], lhs, s16.t[:, s, 256 * r2:256 * r2 + 256], start=z == 0, stop=last),
                        [a] + ms.free, s_msg if last else None)
                ph.free = [g]
                if i == 3:
                    s16.free = [g]
                u = dve(lambda e: e.scalar_tensor_tensor(
                    out=hp.t[:, i, :], in0=ms.t[:, 0:256], scalar=at.t[:, 13:14], in1=hp.t[:, i, :],
                    op0=ALU.mult, op1=ALU.add), [g, hm, rr], s_bl)
                ms.free = [u]
                at.free = [u]
                u = pool(lambda e: e.tensor_tensor(hp.t[:, i, :], hp.t[:, i, :], gain, ALU.mult),
                         [u, tok["gain"]], s_pb)
                bl.append(pool(lambda e: e.tensor_tensor(hp.t[:, i, :], hp.t[:, i, :], bias[:], ALU.add),
                               [u, ld_bi], s_pb))

            bl = []
            rows = []
            for s in range(14):
                if s % 3 == 0 and s < 12:
                    rows.append(row(s // 3))
                for g in list(rows):
                    try:
                        next(g)
                    except StopIteration:
                        rows.remove(g)
                yield
            assert not rows and len(bl) == 4
            yield
            ge = act(lambda e: e.activation(hp.t[:], hp.t[:], ACT.Gelu), bl, s_gelu)
            yield
            for j in range(4):
                x_ready[4 * b + j] = dve(lambda e, j=j: e.scalar_tensor_tensor(
                    out=X[:, 4 * b + j, :], in0=hp.t[:, j, :], scalar=K[:, 6:7], in1=X[:, 4 * b + j, :],
                    op0=ALU.mult, op1=ALU.add), [ge], s_x)
            hp.free = [x_ready[4 * b + 3]]
            tok["attended", b] = True

        class Side:
            def __init__(self):
                self.streams = []

            def step(self):
                for g in list(self.streams):
                    try:
                        next(g)
                    except StopIteration:
                        self.streams.remove(g)

            def finish(self):
                while self.streams:
                    self.step()

        recs = {}

        def attention_stream(c):
            for b in range(4 * c, 4 * c + 4):
                while ("normed", b) not in tok:
                    yield
                yield from attend(b, recs[b], B[0], B[4])

        def router_stream(L, c, turn):
            if L == 1:
                while ("done", 0, c) not in tok:
                    yield
                for b in range(4 * c, 4 * c + 4):
                    yield from combine(0, c, 4 * b)
                    recs[b] = Rec()
                    yield from norm(4 * b, recs[b])
                    tok["normed", b] = True
                    if b > 4 * c:
                        while ("attended", b - 1) not in tok:
                            yield
                        yield from router(1, c, b - 1 - 4 * c, B[7], turn)
                while ("attended", 4 * c + 3) not in tok:
                    yield
                yield from router(1, c, 3, B[7], turn)
            else:
                for g in range(NG):
                    yield from router(0, c, g, B[7], turn)
            yield from tables(L, c, B[7])
            turn["route"] = TURNS[TURNS.index((L, c)) + 1] + (0,) if (L, c) != TURNS[-1] else None

        def final_stream(c):
            while ("done", 1, c) not in tok:
                yield
            for t0 in range(c * NTC, c * NTC + NTC, 4):
                yield from combine(1, c, t0)
                tok["out"] = sp(lambda e, t0=t0: e.dma_start(ov[:, t0:t0 + 4, :], X[:, t0:t0 + 4, :]),
                                [x_ready[t0 + 3]], d_o)

        k_mix = sb("k_mix", [128, 1], F32)
        tab_free = []
        NG = NTC // 4
        TURNS = [(L, c) for L in range(2) for c in range(C)]
        turn = {"route": (0, 0, 0)}

        def first(g):
            yield from router(0, 0, g, B[4 + g], turn)

        mx = maxima()
        side = Side()
        side.streams = [first(0)]
        n = 0
        while side.streams or n < 40:
            if n in (6, 12, 18):
                side.streams.append(first(n // 6))
            side.step()
            next(mx, None)
            n += 1
        for _ in mx:
            pass
        side.streams = [tables(0, 0, B[7])]
        side.finish()
        turn["route"] = (0, 1, 0)
        split()
        split_qk()
        tok["ks"] = scalars()
        tok["ks"] = dve(lambda e: e.tensor_scalar(k_mix[:], K[:, 4:5], 2.0 ** -10, None, ALU.mult), [tok["ks"]], s_kd)

        def in_turn():
            yield from router_stream(0, 1, turn)
            for c in range(C):
                yield from router_stream(1, c, turn)

        def attentions():
            for c in range(C):
                yield from attention_stream(c)

        def finals():
            for c in range(C):
                yield from final_stream(c)

        side.streams = [attentions(), in_turn(), finals()]
        experts(side)
        side.finish()
        sp(lambda e: e.drain(), [tok["out"]] + [(s, s.n) for s in d_y] + z_rows)
        pool(lambda e: e.drain(), [(s, s.n) for s in d_sc] + [(d_pad, d_pad.n)])

        @block.sync
        def _(e):
            Q.emit("sync", e)

        @block.gpsimd
        def _(e):
            Q.emit("gpsimd", e)

        @block.scalar
        def _(e):
            Q.emit("scalar", e)

        @block.tensor
        def _(e):
            Q.emit("tensor", e)

        @block.vector
        def _(e):
            Q.emit("vector", e)


def program(nc, arrays):
    args = {}
    for name, a in arrays.items():
        args[name] = nc.dram_tensor(name, a.shape, mybir.dt.from_np(a.dtype), kind="ExternalInput").ap()
    out = nc.dram_tensor("out", (T, D), F32, kind="ExternalOutput").ap()
    hs = [[nc.dram_tensor(f"hs{l}{c}", (ROWS, 2 * D), F16, kind="Internal").ap() for c in range(C)] for l in range(2)]
    ys = [[nc.dram_tensor(f"ys{l}{c}", (NJ * 128, D), F32, kind="Internal").ap() for c in range(C)] for l in range(2)]
    macaron_kernel(nc, args["x"], args["wk"], args["wqk"], args["gw"], args["gain"], args["bias"], args["lg"],
                   out, hs, ys)


def layout(inputs):
    import numpy as np

    x = np.ascontiguousarray(np.asarray(inputs["L0_attn_x"]).reshape(T, D))
    w1 = np.asarray(inputs["L0_ffn_w1"]).transpose(0, 2, 1).reshape(NE, 2, 128, 512)
    w3 = np.asarray(inputs["L0_ffn_w3"]).transpose(0, 2, 1).reshape(NE, 2, 128, 512)
    w2 = np.asarray(inputs["L0_ffn_w2"]).transpose(0, 2, 1).reshape(NE, 4, 128, 256)
    up = np.concatenate([w1, w3], axis=3).transpose(2, 0, 1, 3).reshape(128, 16, 1024)
    down = w2.transpose(2, 0, 1, 3).reshape(128, 8, 1024)
    wk = np.ascontiguousarray(np.concatenate([up, down], axis=1))
    qk = np.concatenate([np.asarray(inputs["L0_attn_W_q"]), np.asarray(inputs["L0_attn_W_k"])], axis=0)
    wqk = np.ascontiguousarray(qk.T.reshape(2, 128, 64).transpose(1, 0, 2))
    gw = np.ascontiguousarray(np.asarray(inputs["L0_ffn_gate_w"]).T.reshape(2, 128, 8).transpose(1, 0, 2))
    gain = np.ascontiguousarray(np.broadcast_to(np.asarray(inputs["L0_attn_gain"])[None, :], (128, D)))
    bias = np.ascontiguousarray(np.broadcast_to(np.asarray(inputs["L0_attn_bias"])[None, :], (128, D)))
    lg = np.stack([np.asarray(inputs["L0_attn_log_mix"]), np.asarray(inputs["L0_attn_log_scale"])])
    lg = np.ascontiguousarray(np.broadcast_to(lg[None, :], (128, 2)))
    return {"x": x, "wk": wk, "wqk": wqk, "gw": gw, "gain": gain, "bias": bias, "lg": lg}


def kernel(**inputs):
    import concourse.bacc as bacc
    from concourse.bass_utils import run_bass_kernel_spmd

    nc = bacc.Bacc("TRN2", target_bir_lowering=False, num_devices=1)
    arrays = layout(inputs)
    program(nc, arrays)
    r = run_bass_kernel_spmd(nc, [arrays], core_ids=[0])
    return r.results[0]["out"].reshape(8, 512, D)
```

```python
from contextlib import ExitStack

import concourse.bass as bass
from concourse import mybir

ALU = mybir.AluOpType
ACT = mybir.ActivationFunctionType
AX = mybir.AxisListType
F32 = mybir.dt.float32
F16 = mybir.dt.float16
BF16 = mybir.dt.bfloat16
I32 = mybir.dt.int32

T = 4096
D = 256
NE = 8
NT = T // 128
C = 2
NTC = NT // C
CAP = NTC * 128 + 128
NJ = 2 * NTC + NE - 1
SPARE = NE * CAP
ROWS = SPARE + 128
W2OFF = 16 * 2048
ROWGAP = 6
SUBGAP = 4
M0 = 16
SPLIT = 18
NEG = -(2.0 ** 100)
MARK = 2.0 ** 90
EXPO = 0x7F800000
ORDER = ("sync", "gpsimd", "scalar", "tensor", "vector")


class Sem:

    def __init__(self, handle, k=1):
        self.h, self.k, self.n = handle, k, 0


class Slot:

    def __init__(self, t):
        self.t, self.free, self.held = t, [], False

    def take(self):
        while self.held:
            yield
        self.held = True

    def give(self, free):
        self.free, self.held = free, False


class Ring:
    def __init__(self, slots):
        self.slots, self.i = slots, -1

    def next(self):
        self.i = (self.i + 1) % len(self.slots)
        return self.slots[self.i]

    def take(self):
        while all(s.held for s in self.slots):
            yield
        while self.next().held:
            pass
        self.slots[self.i].held = True
        return self.slots[self.i]


class Rec:
    pass


def gap(n):
    for _ in range(n):
        yield


class Queues:

    def __init__(self):
        self.q = {e: [] for e in ORDER}

    def do(self, eng, fn, waits=(), inc=None):
        self.q[eng].append((list(waits), fn, inc))
        if inc is None:
            return None
        inc.n += inc.k
        return (inc, inc.n)

    def emit(self, name, eng):
        seen = {}
        for waits, fn, inc in self.q[name]:
            need = {}
            for s, v in waits:
                need[s] = max(need.get(s, 0), v)
            for s, v in need.items():
                if seen.get(s, 0) < v:
                    eng.wait_ge(s.h, v)
                    seen[s] = v
            ins = fn(eng)
            if inc is not None:
                ins.then_inc(inc.h, inc.k)


def macaron_kernel(nc, x_d, wk_d, wqk_d, gw_d, gain_d, bias_d, lg_d, out_d, hs_d, ys_d):
    with ExitStack() as ctx:
        def sb(name, shape, dt):
            return ctx.enter_context(nc.sbuf_tensor("t_" + name, shape, dt))

        def sem(name, k=1):
            return Sem(ctx.enter_context(nc.semaphore(name)), k)

        Q = Queues()
        do = Q.do

        def pe(fn, waits=(), inc=None):
            return do("tensor", fn, waits, inc)

        def dve(fn, waits=(), inc=None):
            return do("vector", fn, waits, inc)

        def act(fn, waits=(), inc=None):
            return do("scalar", fn, waits, inc)

        def pool(fn, waits=(), inc=None):
            return do("gpsimd", fn, waits, inc)

        def sp(fn, waits=(), inc=None):
            return do("sync", fn, waits, inc)

        W = sb("W", [128, 26, 1024], F32)
        W16 = W[:, :, :].rearrange("p a b -> p (a b)").bitcast(F16)
        X = sb("X", [128, NT, D], F32)
        identf = sb("identf", [128, 128], F32)
        ident16 = sb("ident16", [128, 128], F16)
        identb = sb("identb", [128, 128], BF16)
        ones16 = sb("ones16", [128, 128], F16)
        tri = sb("tri", [128, 128], F16)
        maskf = sb("maskf", [128, 128], F32)
        maskb = sb("maskb", [128, 128], BF16)
        row0 = sb("row0", [128, 128], F16)
        extra0 = sb("extra0", [128, 1], F32)
        mhalf = sb("mhalf", [128, 4], F32)
        zrow = sb("zrow", [128, 512], F16)
        ebi = sb("ebi", [128, 8], I32)
        ebase = sb("ebase", [128, 8], F32)
        ebpi = sb("ebpi", [128, 8], I32)
        ebp = sb("ebp", [128, 8], F32)
        tie = sb("tie", [128, 8], F32)
        tiei = sb("tiei", [128, 8], I32)
        jioi = sb("jioi", [128, 8], I32)
        jio = sb("jio", [128, 8], F32)
        gain = W[:, 24, 3 * D:4 * D]
        bias = sb("bias", [128, D], F32)
        gw = sb("gw", [128, 2, 8], F32)
        wqk = sb("wqk", [128, 2, 64], F32)
        WQ = sb("WQ", [128, 2, 2, 2, 96], F16)
        lg = sb("lg", [128, 2], F32)
        lt = sb("lt", [128, 8], F32)
        M3 = sb("M3", [128, 3], F32)
        MC = sb("MC", [3, 1], F32)
        MD = sb("MD", [3, 3], F32)
        MO = sb("MO", [3, 128], F32)
        MP = sb("MP", [128, 3], F32)
        SC = sb("SC", [128, 3], F32)
        K = sb("K", [128, 8], F32)
        HP = Ring([Slot(sb(f"hp{i}", [128, 4, D], F32)) for i in range(3)])
        S16 = Ring([Slot(sb(f"s16{i}", [128, 4, 512], F16)) for i in range(3)])
        BS = Ring([Slot(sb(f"bs{i}", [128, 4, 6], F32)) for i in range(3)])
        MV = Ring([Slot(sb(f"mv{i}", [128, 4, 2], F32)) for i in range(3)])
        VE = Ring([Slot(sb(f"ve{i}", [128, 2, 4], F32)) for i in range(3)])
        HT32 = Slot(sb("ht32", [128, 512], F32))
        rta = sb("rta", [128, 6 * NTC * 8], F32)
        rsa = sb("rsa", [128, 8 * NTC], F32)
        m16a = sb("m16a", [128, NTC * 8], F16)

        def routing(i, n):
            return Slot((rta[:, 48 * n * i:48 * n * (i + 1)].rearrange("p (q t e) -> p q t e", q=6, e=8),
                         rsa[:, 8 * n * i:8 * n * (i + 1)].rearrange("p (q t) -> p q t", q=8),
                         m16a[:, 8 * n * i:8 * n * (i + 1)].rearrange("p (t e) -> p t e", e=8)))

        RW = {n: Ring([routing(i, n) for i in range(NTC // n)]) for n in (8, 4)}
        CP = sb("CP", [128, NTC + 1, 8], F16)
        POS = sb("POS", [128, 2, 2, NT], I32)
        POSY = sb("POSY", [128, 2, 2, NT], I32)
        OH = sb("OH", [128, 2, NTC, 8], F16)
        OF = sb("OF", [128, 2, NTC, 8], F32)
        OS = sb("OS", [128, 2, NTC], F32)
        oh_free = []
        tok = {}
        DL = sb("DL", [128, 8], F32)
        CW = sb("CW", [128, 2, 2, NT], F32)
        TT = sb("TT", [128, 6, 8], F32)
        NTI = sb("NTI", [128, 8], I32)
        PADI = sb("PADI", [128, 8], I32)
        TJ = sb("TJ", [NJ, 2, 8], F32)
        TR = sb("TR", [NJ, 4], F32)
        TAB = [[sb(f"tab{l}{c}", [NJ, 2], I32) for c in range(C)] for l in range(2)]
        HTA = Slot(sb("hta", [128, 4, 512], F16))
        S16H = Ring(S16.slots + [HTA])
        QS = Slot(sb("QS", [96, 512], F16))
        KS = Slot(sb("KS", [96, 512], F16))
        SIM = Ring([Slot(sb(f"sim{i}", [128, 512], F32)) for i in range(2)])
        PH = Ring([Slot(sb(f"ph{i}", [128, 2, 512], F16)) for i in range(2)])
        wqh = PH.slots[0].t[:, 0, 0:128].rearrange("p (a b) -> p a b", a=2)
        wql = PH.slots[0].t[:, 0, 128:256].rearrange("p (a b) -> p a b", a=2)
        AT = Ring([Slot(sb(f"at{i}", [128, 16], F32)) for i in range(4)])
        HT = Ring([Slot(sb(f"ht{i}", [128, 512], F16)) for i in range(3)])
        TH = Ring([Slot(sb(f"th{i}", [128, 512], F32)) for i in range(2)])
        GP = Ring([Slot(sb(f"gp{i}", [128, 2, 512], F16)) for i in range(2)])
        GH = Ring([Slot(sb(f"gh{i}", [128, 2, 512], F16)) for i in range(2)])
        YO = Ring([Slot(W[:, 24, D * i:D * i + D]) for i in range(3)])
        YG = Ring([Slot(W[:, 25, 512 * i:512 * i + 512].rearrange("p (k d) -> p k d", k=2)) for i in range(2)])

        B = [Slot(ctx.enter_context(nc.psum_tensor(f"B{i}", [128, 512], F32))) for i in range(8)]

        d_x = [sem(f"d_x{i}", 16) for i in range(8)]
        d_w = [sem(f"d_w{i}", 16) for i in range(6)]
        d_c = [sem(f"d_c{i}", 16) for i in range(5)]
        d_in = [sem(f"d_in{i}", 16) for i in range(4)]
        d_y = [sem(f"d_y{i}", 16) for i in range(3)]
        d_sc = [sem(f"d_sc{i}", 16) for i in range(4)]
        d_h = sem("d_h", 16)
        d_gt = [sem(f"d_gt{i}", 16) for i in range(2)]
        d_pad = sem("d_pad", 16)
        d_z = sem("d_z", 16)
        d_g = [sem(f"d_g{i}", 16) for i in range(2)]
        d_o = sem("d_o", 16)
        s_k = sem("s_k")
        s_kd = sem("s_kd")
        s_ka = sem("s_ka")
        s_wh = sem("s_wh")
        s_wl = sem("s_wl")
        s_mx = sem("s_mx")
        s_ma = sem("s_ma")
        s_pm = sem("s_pm")
        s_ln = sem("s_ln")
        s_pw = sem("s_pw")
        s_hh = sem("s_hh")
        s_tp = sem("s_tp")
        s_tc = sem("s_tc")
        s_gs = sem("s_gs")
        s_rt = sem("s_rt")
        s_e2 = sem("s_e2")
        s_rk = sem("s_rk")
        s_tab = sem("s_tab")
        s_tin = sem("s_tin")
        s_ht = sem("s_ht")
        s_x1 = sem("s_x1")
        s_x3 = sem("s_x3")
        s_th = sem("s_th")
        s_g = sem("s_g")
        s_gh = sem("s_gh")
        s_gl = sem("s_gl")
        s_y = sem("s_y")
        s_yc = sem("s_yc")
        s_x = sem("s_x")
        s_at = sem("s_at")
        s_ac = sem("s_ac")
        s_sim = sem("s_sim")
        s_sco = sem("s_sco")
        s_top = sem("s_top")
        s_p = sem("s_p")
        s_pt = sem("s_pt")
        s_ps = sem("s_ps")
        s_msg = sem("s_msg")
        s_bl = sem("s_bl")
        s_pb = sem("s_pb")
        s_gelu = sem("s_gelu")

        block = ctx.enter_context(nc.Block())

        k1 = pool(lambda e: e.memset(identf[:], 0.0), inc=s_k)
        k2 = pool(lambda e: e.memset(ones16[:], 1.0), inc=s_k)
        k3 = pool(lambda e: e.memset(maskf[:], 0.0), inc=s_k)
        pool(lambda e: e.memset(row0[:], 0.0), inc=s_k)
        pool(lambda e: e.memset(extra0[:], 0.0), inc=s_k)
        pool(lambda e: e.memset(mhalf[:], -0.5), inc=s_k)
        k_half = (s_k, s_k.n)
        k_one = pool(lambda e: e.memset(MO[:], 1.0), inc=s_k)
        pool(lambda e: e.memset(zrow[:], 0.0), inc=s_k)
        pool(lambda e: e.iota(ebi[:], pattern=[[CAP, 8]], base=0, channel_multiplier=0), inc=s_k)
        pool(lambda e: e.iota(ebpi[:], pattern=[[CAP, 8]], base=0, channel_multiplier=1), inc=s_k)
        pool(lambda e: e.iota(tiei[:], pattern=[[-1, 8]], base=8, channel_multiplier=0), inc=s_k)
        pool(lambda e: e.iota(jioi[:], pattern=[[0, 8]], base=0, channel_multiplier=1), inc=s_k)
        kz = (s_k, s_k.n)
        pool(lambda e: e.affine_select(out=identf[:], in_=identf[:], compare_op=ALU.not_equal, fill=1.0, base=0,
                                       pattern=[[-1, 128]], channel_multiplier=1), [kz], s_k)
        pool(lambda e: e.affine_select(out=tri[:], in_=ones16[:], compare_op=ALU.is_gt, fill=0.0, base=0,
                                       pattern=[[1, 128]], channel_multiplier=-1), [kz], s_k)
        pool(lambda e: e.affine_select(out=maskf[:], in_=maskf[:], compare_op=ALU.is_gt, fill=NEG, base=0,
                                       pattern=[[-1, 128]], channel_multiplier=1), [kz], s_k)
        pool(lambda e: e.affine_select(out=extra0[:], in_=extra0[:], compare_op=ALU.not_equal, fill=384.0, base=0,
                                       pattern=[[0, 1]], channel_multiplier=1), [kz], s_k)
        pool(lambda e: e.memset(row0[:, 0:1], 2.0 ** 14), [kz], s_k)
        kc = (s_k, s_k.n)
        for a, b in ((ident16, identf), (identb, identf), (maskb, maskf), (ebase, ebi), (ebp, ebpi),
                     (tie, tiei), (jio, jioi)):
            dve(lambda e, a=a, b=b: e.tensor_copy(a[:], b[:]), [kc], s_kd)
        kd = (s_kd, s_kd.n)

        xv = x_d.rearrange("(n p) d -> p n d", p=128)
        ov = out_d.rearrange("(n p) d -> p n d", p=128)
        def load_x(i):
            return sp(lambda e: e.dma_start(X[:, 4 * i:4 * i + 4, :], xv[:, 4 * i:4 * i + 4, :]), inc=d_x[i])

        x_loads = [load_x(0)]
        ld_gw = sp(lambda e: e.dma_start(gw[:], gw_d), inc=d_c[0])
        ld_qk = sp(lambda e: e.dma_start(wqk[:], wqk_d), inc=d_c[1])
        ld_lg = sp(lambda e: e.dma_start(lg[:], lg_d), inc=d_c[2])
        x_loads += [load_x(i) for i in range(1, 4)]
        w_ready = []
        for i in range(6):
            w_ready.append(sp(lambda e, i=i: e.dma_start(W[:, 4 * i + 2:4 * i + 6, :], wk_d[:, 4 * i:4 * i + 4, :]),
                              inc=d_w[i]))
        x_loads += [load_x(i) for i in range(4, 8)]
        x_ready = [x_loads[i // 4] for i in range(NT)]
        ld_bi = sp(lambda e: e.dma_start(bias[:], bias_d), inc=d_c[4])
        z_rows = []
        for l in range(2):
            for c in range(C):
                z_rows.append(sp(lambda e, l=l, c=c: e.dma_start(hs_d[l][c][SPARE:SPARE + 128, :], zrow[:]),
                                 [kz], d_z))

        def maxima():
            t = dve(lambda e: e.tensor_reduce(M3[:, 2:3], wqk[:].rearrange("p a b -> p (a b)"), AX.X, ALU.max,
                                              apply_absolute_value=True), [ld_qk], s_mx)
            part = [W[:, i // 2, 512 * (i % 2):512 * (i % 2) + 512].bitcast(BF16) for i in range(4)]
            ab = [Slot(part[2]), Slot(part[3])]
            top = t
            for k in range(24):
                a = ab[k % 2]
                d = act(lambda e, k=k, a=a: e.activation(a.t, W[:, k + 2, :], ACT.Abs), [w_ready[k // 4]] + a.free, s_ma)
                run = part[k // 16]
                if k in (0, 16):
                    top = dve(lambda e, a=a, run=run: e.tensor_copy(run, a.t), [d], s_mx)
                else:
                    top = dve(lambda e, a=a, run=run: e.tensor_tensor(run, run, a.t, ALU.max), [d, top], s_mx)
                a.free = [top]
                if k in (15, 23):
                    top = dve(lambda e, k=k, run=run: e.tensor_reduce(M3[:, k // 16:k // 16 + 1], run, AX.X, ALU.max),
                              [top], s_mx)
                yield
            a = top
            bank = B[3]
            a = pe(lambda e: e.transpose(bank.t[0:3, 0:128], M3[:], identf[:]), [a, kd] + bank.free, s_pm)
            a = dve(lambda e: e.tensor_reduce(MC[:, 0:1], bank.t[0:3, 0:128], AX.X, ALU.max), [a], s_mx)
            a = dve(lambda e: e.tensor_scalar(MC[:, 0:1], MC[:, 0:1], 2.0 ** -30, None, ALU.max), [a], s_mx)
            a = dve(lambda e: e.tensor_scalar(MC[:, 0:1].bitcast(I32), MC[:, 0:1].bitcast(I32), EXPO, None,
                                              ALU.bitwise_and), [a], s_mx)
            a = dve(lambda e: e.tensor_scalar(MD[:], identf[0:3, 0:3], MC[:, 0:1], None, ALU.mult), [a], s_mx)
            a = pe(lambda e: e.matmul(bank.t[:, 0:3], MO[:], MD[:], start=True, stop=True), [a, k_one], s_pm)
            b = dve(lambda e: e.tensor_copy(MP[:], bank.t[:, 0:3]), [a], s_mx)
            bank.free = [b]
            b = dve(lambda e: e.tensor_scalar(SC[:].bitcast(I32), MP[:].bitcast(I32), -1.0, float(268 << 23),
                                              ALU.mult, ALU.add), [b], s_mx)
            dve(lambda e: e.tensor_scalar(K[:, 0:1], MP[:, 0:1], 2.0 ** -25, None, ALU.mult), [b], s_mx)
            dve(lambda e: e.tensor_scalar(K[:, 1:2], MP[:, 0:1], MP[:, 0:1], MP[:, 1:2], ALU.mult, ALU.mult), [b], s_mx)
            a = dve(lambda e: e.tensor_scalar(K[:, 2:3], MP[:, 2:3], MP[:, 2:3], 2.0 ** -12 / 32 ** 0.5,
                                              ALU.mult, ALU.mult), [b], s_mx)
            dve(lambda e: e.tensor_scalar(K[:, 1:2], K[:, 1:2], 2.0 ** -12, None, ALU.mult), [a], s_mx)
            tok["kk"] = dve(lambda e: e.tensor_scalar(K[:, 3:4], K[:, 2:3], -1.0, None, ALU.mult), [a], s_mx)

        def split():
            scaled = tok["kk"]
            l = [None] * 24
            h = [None] * 24
            for k in range(24):
                o = k * 2048
                s = SC[:, 0:1] if k < 16 else SC[:, 1:2]
                w = [scaled]
                if k >= 2:
                    w.append(l[k - 2])
                h[k] = act(lambda e, k=k, o=o, s=s: e.activation(W16[:, o:o + 1024], W[:, k + 2, :], ACT.Copy,
                                                                 scale=s), w, s_wh)
                l[k] = dve(lambda e, k=k, o=o, s=s: e.scalar_tensor_tensor(
                    out=W16[:, o + 1024:o + 2048], in0=W[:, k + 2, :], scalar=s, in1=W16[:, o:o + 1024],
                    op0=ALU.mult, op1=ALU.subtract), [h[k]], s_wl)
                tok["w13"] = l[min(k, 15)]
                yield
            tok["w"] = l[23]
            for slot in YO.slots + YG.slots:
                slot.free = [l[23]]

        def split_qk():
            a = dve(lambda e: e.tensor_scalar(wqh, wqk[:], SC[:, 2:3], None, ALU.mult), [tok["kk"]], s_wl)
            a = dve(lambda e: e.scalar_tensor_tensor(out=wql, in0=wqk[:], scalar=SC[:, 2:3], in1=wqh,
                                                     op0=ALU.mult, op1=ALU.subtract), [a], s_wl)
            for r in range(3):
                for m in range(2):
                    dve(lambda e, r=r, m=m: e.tensor_copy(WQ[:, :, 0, m, 32 * r:32 * r + 32],
                                                          wqh[:, :, 32 * m:32 * m + 32]), [a], s_wl)
                    w = dve(lambda e, r=r, m=m: e.tensor_copy(WQ[:, :, 1, m, 32 * r:32 * r + 32],
                                                              wql[:, :, 32 * m:32 * m + 32]), [a], s_wl)
            tok["wq"] = w

        def scalars():
            a = act(lambda e: e.activation(lt[:, 0:1], lg[:, 0:1], ACT.Tanh, scale=0.5), [ld_lg], s_ka)
            b = dve(lambda e: e.tensor_scalar(lt[:, 1:2], lg[:, 1:2], -1.0, None, ALU.mult), [ld_lg], s_kd)
            b = dve(lambda e: e.tensor_tensor(lt[:, 2:3], lt[:, 1:2], lg[:, 1:2], ALU.min), [b], s_kd)
            b = act(lambda e: e.activation(lt[:, 3:4], lt[:, 2:3], ACT.Exp), [b], s_ka)
            b = dve(lambda e: e.tensor_scalar(lt[:, 4:5], lt[:, 3:4], 1.0, None, ALU.add), [b], s_kd)
            b = act(lambda e: e.activation(lt[:, 5:6], lt[:, 4:5], ACT.Ln), [b], s_ka)
            c = dve(lambda e: e.tensor_scalar(lt[:, 6:7], lg[:, 1:2], 0.0, 0.01, ALU.max, ALU.add), [b], s_kd)
            dve(lambda e: e.tensor_tensor(K[:, 6:7], lt[:, 5:6], lt[:, 6:7], ALU.add), [c], s_kd)
            dve(lambda e: e.tensor_scalar(K[:, 4:5], lt[:, 0:1], 0.5, 0.5, ALU.mult, ALU.add), [a], s_kd)
            return dve(lambda e: e.tensor_scalar(K[:, 5:6], lt[:, 0:1], -0.5, 0.5, ALU.mult, ALU.add), [a], s_kd)

        def norm(t0, r, ring=S16):
            hp = yield from HP.take()
            s16 = yield from ring.take()
            r.hp, r.s16, r.sc_sem = hp, s16, d_sc[ring.i]
            bs, mv, ve = BS.next(), MV.next(), VE.next()
            for j in range(4):
                a = dve(lambda e, j=j: e.bn_stats(bs.t[:, j, :], X[:, t0 + j, :]), [x_ready[t0 + j]] + bs.free, s_ln)
                bs.free = []
                if j == 1:
                    yield from gap(1)
            yield from gap(1)
            st = a
            for j in range(4):
                a = dve(lambda e, j=j: e.bn_aggr(mv.t[:, j, :], bs.t[:, j, :]), [st] + mv.free, s_ln)
                mv.free = []
            a = dve(lambda e: e.tensor_scalar(ve.t[:, 0, :], mv.t[:, :, 1], 1e-5, 2.0 ** -20, ALU.add, ALU.mult),
                    [a] + ve.free, s_ln)
            p = pool(lambda e: e.tensor_tensor(ve.t[:, 1, :], ve.t[:, 0, :], mhalf[:], ALU.pow), [a, k_half], s_pw)
            yield from gap(3)
            r.hp_t, hh_t, r.hl_t = [], [], []
            for j in range(4):
                r.hp_t.append(dve(lambda e, j=j: e.tensor_scalar(
                    hp.t[:, j, :], X[:, t0 + j, :], mv.t[:, j, 0:1], ve.t[:, 1, j:j + 1],
                    ALU.subtract, ALU.mult), [p] + hp.free, s_ln))
                hh_t.append(act(lambda e, j=j: e.activation(s16.t[:, j, 0:256], hp.t[:, j, :], ACT.Copy),
                                [r.hp_t[j]] + s16.free, s_hh))
            yield from gap(4)
            for j in range(4):
                r.hl_t.append(dve(lambda e, j=j: e.tensor_tensor(s16.t[:, j, 256:512], hp.t[:, j, :],
                                                                 s16.t[:, j, 0:256], ALU.subtract),
                                  [hh_t[j]], s_ln))
                if j == 1:
                    yield from gap(1)
            bs.free, mv.free, ve.free = [r.hl_t[-1]], [r.hl_t[-1]], [r.hl_t[-1]]

        def gate_scores(t0, r, tb, gb, o, ring):
            yield from norm(t0, r, ring)
            hp = r.hp
            yield from gap(1)
            for h in range(2):
                yield from HT32.take()
                for j in (2 * h, 2 * h + 1):
                    for b in range(2):
                        p = 256 * (j % 2) + 128 * b
                        tp = pe(lambda e, j=j, b=b, p=p: e.transpose(
                            tb.t[:, p:p + 128], hp.t[:, j, 128 * b:128 * b + 128], identf[:]),
                            [r.hp_t[j], kd] + tb.free, s_tp)
                tc = act(lambda e: e.activation(HT32.t[:], tb.t[:], ACT.Copy), [tp] + HT32.free, s_tc)
                tb.free = [tc]
                yield from gap(2)
                for j in (2 * h, 2 * h + 1):
                    for b in range(2):
                        p = 256 * (j % 2) + 128 * b
                        gs = pe(lambda e, j=j, b=b, p=p: e.matmul(
                            gb.t[:, o + 8 * j:o + 8 * j + 8], HT32.t[:, p:p + 128], gw[:, b, :],
                            start=b == 0, stop=b == 1), [tc, ld_gw] + gb.free, s_gs)
                HT32.give([gs])
            r.gs = gs
            hp.give([tp, r.hl_t[-1]])

        def first_routers(c, banks, tbs, spawn):
            subs = [Rec() for s in range(NTC // 4)]
            for s, r in enumerate(subs):
                spawn(gate_scores(c * NTC + 4 * s, r, tbs[s % len(tbs)], banks[s // 2], 32 * (s % 2), S16H))
                yield from gap(SUBGAP)
            for g in range(NTC // 8):
                yield from router(0, c, g, 8, banks[g], subs[2 * g:2 * g + 2])

        def router(L, c, g, n, bank, rs4):
            t0 = c * NTC + n * g
            while not all(hasattr(r, "gs") for r in rs4):
                yield
            rw = RW[n].next()
            R, S, M = rw.t
            sc = dve(lambda e: e.tensor_copy(R[:, 0], bank.t[:, 0:8 * n].rearrange("p (a b) -> p a b", b=8)),
                     [rs4[-1].gs] + rw.free, s_rt)
            bank.free = [sc]
            yield from gap(2)

            def bc(ap):
                return ap.unsqueeze(2).to_broadcast([128, n, 8])

            tieb = tie[:].unsqueeze(1).to_broadcast([128, n, 8])
            chain = [sc]

            def step(fn):
                t = dve(fn, list(chain), s_rt)
                chain[:] = [t]
                return t

            for k, (src, oh) in enumerate(((0, 2), (3, 4))):
                step(lambda e, src=src, k=k: e.tensor_reduce(S[:, k], R[:, src], AX.X, ALU.max))
                step(lambda e, src=src, k=k: e.tensor_tensor(R[:, 1], R[:, src], bc(S[:, k]), ALU.is_equal))
                step(lambda e: e.tensor_tensor(R[:, 1], R[:, 1], tieb, ALU.mult))
                step(lambda e: e.tensor_reduce(S[:, 2], R[:, 1], AX.X, ALU.max))
                step(lambda e, oh=oh: e.tensor_tensor(R[:, oh], R[:, 1], bc(S[:, 2]), ALU.is_equal))
                if k == 0:
                    step(lambda e: e.scalar_tensor_tensor(out=R[:, 3], in0=R[:, 2], scalar=-3e38, in1=R[:, 0],
                                                          op0=ALU.mult, op1=ALU.add))
                    yield from gap(1)
            df = step(lambda e: e.tensor_tensor(S[:, 3], S[:, 1], S[:, 0], ALU.subtract))
            ex = act(lambda e: e.activation(S[:, 4], S[:, 3], ACT.Exp, scale=2.0 ** -10), [df], s_e2)
            mm = step(lambda e: e.tensor_tensor(M, R[:, 2], R[:, 4], ALU.add))
            if g == 0:
                step(lambda e: e.memset(CP[:, 0, :], 0.0))
            for j in range(n):
                cp = step(lambda e, j=j: e.tensor_tensor(CP[:, n * g + j + 1, :], CP[:, n * g + j, :],
                                                         M[:, j, :], ALU.add))
            chain.extend(oh_free)
            for k, oh in enumerate((2, 4)):
                step(lambda e, oh=oh, k=k: e.tensor_copy(OH[:, k, n * g:n * g + n, :], R[:, oh]))
            yield from gap(3)
            pe(lambda e: e.matmul(bank.t[:, 0:8 * n], tri[:], M.rearrange("p a b -> p (a b)"),
                                  start=True, stop=False), [mm, kd] + bank.free)
            rk = pe(lambda e: e.matmul(bank.t[:, 0:8 * n], ones16[:], CP[:, n * g:n * g + n, :].rearrange(
                "p a b -> p (a b)"), start=False, stop=True), [cp], s_rk)
            yield from gap(2)
            chain.append(rk)
            rb = step(lambda e: e.tensor_tensor(R[:, 5], bank.t[:, 0:8 * n].rearrange("p (a b) -> p a b", b=8),
                                                ebase[:].unsqueeze(1).to_broadcast([128, n, 8]), ALU.add))
            bank.free = [rb]
            for k, oh in enumerate((2, 4)):
                step(lambda e, oh=oh: e.tensor_tensor(R[:, oh], R[:, oh], R[:, 5], ALU.mult))

                def total(e, oh=oh, k=k):
                    with nc.allow_low_precision(reason="whole numbers"):
                        return e.tensor_reduce(POS[:, L, k, t0:t0 + n], R[:, oh], AX.X, ALU.add)
                ps = step(total)
            yield from gap(1)
            chain.append(ex)
            step(lambda e: e.tensor_scalar(S[:, 5], S[:, 4], 1.0, None, ALU.add))
            step(lambda e: e.reciprocal(S[:, 6], S[:, 5]))
            step(lambda e: e.tensor_tensor(S[:, 7], S[:, 6], S[:, 4], ALU.mult))
            step(lambda e: e.tensor_copy(CW[:, L, 0, t0:t0 + n], S[:, 6]))
            cw = step(lambda e: e.tensor_copy(CW[:, L, 1, t0:t0 + n], S[:, 7]))
            rw.free = [cw, rk]
            if n == 8:
                for slot in RW[4].slots[2 * g:2 * g + 2]:
                    slot.free = rw.free
            tok["cp"] = cp
            for s, r in enumerate(rs4):
                for j in range(4):
                    for k in range(2):
                        t = t0 + 4 * s + j
                        sd = pool(lambda e, r=r, j=j, k=k, t=t: e.indirect_dma_start(
                            hs_d[L][c], bass.IndirectOffsetOnAxis(ap=POS[:, L, k, t:t + 1], axis=0),
                            r.s16.t[:, j, :], None), [ps, r.hl_t[j]], r.sc_sem)
                r.s16.give([sd])
                tok["scattered", L, c] = tok.get(("scattered", L, c), []) + [sd]

        def tables(L, c, bank):
            cn = pe(lambda e: e.matmul(bank.t[:, 0:8], ones16[:], CP[:, NTC, :], start=True, stop=True),
                    [tok["cp"]] + bank.free, s_rk)
            chain = [cn] + tab_free
            yield from gap(1)

            def step(fn):
                t = dve(fn, list(chain), s_tab)
                chain[:] = [t]
                return t

            ne = step(lambda e: e.tensor_copy(TT[:, 0], bank.t[:, 0:8]))
            bank.free = [ne]
            pi = step(lambda e: e.tensor_tensor(PADI[:], TT[:, 0], ebp[:], ALU.add))
            for i in range(8):
                pd = pool(lambda e, i=i: e.indirect_dma_start(
                    hs_d[L][c], bass.IndirectOffsetOnAxis(ap=PADI[:, i:i + 1], axis=0), zrow[:], None), [pi, kc], d_pad)
            step(lambda e: e.tensor_scalar(NTI[:], TT[:, 0], 127.0, None, ALU.add))
            step(lambda e: e.tensor_scalar(NTI[:], NTI[:], 7, None, ALU.arith_shift_right))
            step(lambda e: e.tensor_copy(TT[:, 1], NTI[:]))
            step(lambda e: e.memset(TT[:, 3], 0.0))
            step(lambda e: e.tensor_tensor_scan(TT[:, 2], TT[:, 1], TT[:, 3], 0.0, ALU.add, ALU.add))
            step(lambda e: e.tensor_tensor(TJ[:, 0], TT[0:NJ, 2], jio[0:NJ], ALU.is_le))
            step(lambda e: e.tensor_tensor(TJ[:, 1], TJ[:, 0], TT[0:NJ, 1], ALU.mult))
            step(lambda e: e.tensor_reduce(TR[:, 0:1], TJ[:, 0], AX.X, ALU.add))
            step(lambda e: e.tensor_reduce(TR[:, 1:2], TJ[:, 1], AX.X, ALU.add))
            step(lambda e: e.tensor_tensor(TR[:, 2:3], jio[0:NJ, 0:1], TR[:, 1:2], ALU.subtract))
            step(lambda e: e.tensor_scalar(TR[:, 2:3], TR[:, 2:3], 128.0, None, ALU.mult))
            step(lambda e: e.scalar_tensor_tensor(out=TR[:, 3:4], in0=TR[:, 0:1], scalar=float(CAP), in1=TR[:, 2:3],
                                                  op0=ALU.mult, op1=ALU.add))
            tab = TAB[L][c]
            step(lambda e: e.tensor_scalar(tab[:, 0:1], TR[:, 0:1], 7.0, None, ALU.min))
            t = step(lambda e: e.tensor_scalar(tab[:, 1:2], TR[:, 3:4], float(SPARE), None, ALU.min))
            tok["table", L, c] = t
            tok["ready", L, c] = tok["scattered", L, c] + [pd, z_rows[-1]]
            yield from gap(1)
            step(lambda e: e.tensor_tensor(DL[:], TT[:, 2], TT[:, 1], ALU.subtract))
            step(lambda e: e.scalar_tensor_tensor(out=DL[:], in0=DL[:], scalar=128.0, in1=ebase[:],
                                                  op0=ALU.mult, op1=ALU.subtract))
            for k in range(2):
                step(lambda e, k=k: e.tensor_tensor(OF[:, k], OH[:, k], DL[:].unsqueeze(1).to_broadcast(
                    [128, NTC, 8]), ALU.mult))
                step(lambda e, k=k: e.tensor_reduce(OS[:, k], OF[:, k], AX.X, ALU.add))
                yp = step(lambda e, k=k: e.tensor_tensor(
                    POSY[:, L, k, c * NTC:c * NTC + NTC], OS[:, k], POS[:, L, k, c * NTC:c * NTC + NTC], ALU.add))
            oh_free[:] = [yp]
            chain.append(tok["kk"])
            t = step(lambda e: e.tensor_scalar(CW[:, L, :, c * NTC:c * NTC + NTC], CW[:, L, :, c * NTC:c * NTC + NTC],
                                               K[:, 1:2], None, ALU.mult))
            tok["ypos", L, c] = t
            tab_free[:] = [t, pd]

        def experts(side):
            seq = [(L, c, j) for L in range(2) for c in range(C) for j in range(NJ)]
            htt, gt, highs, out, expert = {}, {}, {}, {}, {}

            def load(n):
                L, c, j = seq[n]
                tab = TAB[L][c]
                while ("table", L, c) not in tok:
                    side.step()
                h = HT.next()

                def f(e):
                    r = e.value_load(tab[j:j + 1, 1:2], min_val=0, max_val=SPARE)
                    return e.dma_start(h.t[:].rearrange("p (a b) -> p a b", a=4), hs_d[L][c][bass.ds(r, 128), :],
                                       transpose=True)
                t = sp(f, [tok["table", L, c]] + tok["ready", L, c] + h.free, d_in[HT.i])
                htt[n] = (h, t)

            def which(n):
                L, c, j = seq[n]

                def f(e):
                    expert[n] = e.value_load(TAB[L][c][j:j + 1, 0:1], min_val=0, max_val=7)
                pe(f, [tok["table", L, c]])

            def ups(n, w, hold):
                L, c, j = seq[n]
                tab = TAB[L][c]
                h, h_t = htt[n]
                bank, s = (B[1], s_x1) if w == 0 else (B[2], s_x3)
                k = 0
                for db in range(2):
                    if db == 1:
                        side.step()
                    for hl, wl in ((0, 0), (0, 1), (1, 0)):
                        def f(e, db=db, hl=hl, wl=wl, k=k):
                            return e.matmul(bank.t[:], h.t[:, (2 * hl + db) * 128:(2 * hl + db) * 128 + 128],
                                            W16[:, bass.ds(expert[n] * 4096 + (db * 2048 + wl * 1024 + w * 512), 512)],
                                            start=k == 0, stop=k == 5)
                        a = pe(f, [h_t, tok["w13"], tok["table", L, c]] + bank.free, s if k == 5 else None)
                        k += 1
                return a

            def up_a(n, hold):
                x1 = ups(n, 0, hold)
                th = TH.next()
                a = act(lambda e: e.activation(th.t[:], B[1].t[:], ACT.Tanh, scale=K[:, 0:1]),
                        [x1, tok["kk"]] + th.free, s_th)
                hold["a"] = a
                hold["th"] = th

            def up_b(n, hold):
                hold["x3"] = ups(n, 1, hold)
                htt.pop(n)[0].free = [hold["x3"]]

            def gate(n, hold):
                x3, a, th = hold["x3"], hold["a"], hold["th"]
                b = dve(lambda e: e.scalar_tensor_tensor(out=th.t[:], in0=th.t[:], scalar=1.0, in1=B[1].t[:],
                                                         op0=ALU.add, op1=ALU.mult), [a], s_g)
                B[1].free = [b]
                b = dve(lambda e: e.scalar_tensor_tensor(out=th.t[:], in0=B[2].t[:], scalar=2.0 ** -52, in1=th.t[:],
                                                         op0=ALU.mult, op1=ALU.mult), [b, x3], s_g)
                B[2].free = [b]
                gt[n] = (th, b)

            def high(n):
                th, g_t = gt.pop(n)
                gp = GP.next()
                a = act(lambda e: e.activation(gp.t[:, 0, :], th.t[:], ACT.Copy), [g_t] + gp.free, s_gh)
                highs[n] = (th, gp, a)

            def low(n):
                th, gp, a = highs.pop(n)
                gh = GH.next()
                a = dve(lambda e: e.tensor_tensor(gp.t[:, 1, :], th.t[:], gp.t[:, 0, :], ALU.subtract), [a], s_gl)
                th.free = [a]
                t = sp(lambda e: e.dma_start(gh.t[:].rearrange("p a (b c) -> p (a b) c", c=128),
                                             gp.t[:].rearrange("p a b -> p (a b)"), transpose=True),
                       [a] + gh.free, d_gt[GH.i])
                gp.free = [t]
                out[n] = (gh, t)

            def down(n):
                L, c, j = seq[n]
                tab = TAB[L][c]
                gh, a = out.pop(n)
                while "w" not in tok:
                    side.step()
                b = B[4]
                k = 0
                for fb in range(4):
                    if fb == 2:
                        side.step()
                    for gl, wl in ((0, 0), (0, 1), (1, 0)):
                        def f(e, fb=fb, gl=gl, wl=wl, k=k):
                            return e.matmul(b.t[:, 0:256], gh.t[:, gl, fb * 128:fb * 128 + 128],
                                            W16[:, bass.ds(expert[n] * 2048 + (W2OFF + wl * 1024 + fb * 256), 256)],
                                            start=k == 0, stop=k == 11)
                        t = pe(f, [a, tok["w"]] + b.free, s_y if k == 11 else None)
                        k += 1
                gh.free = [t]
                yo = YO.next()
                yc = act(lambda e: e.activation(yo.t, b.t[:, 0:256], ACT.Copy), [t] + yo.free, s_yc)
                b.free = [yc]
                t = sp(lambda e: e.dma_start(ys_d[L][c][128 * j:128 * j + 128, :], yo.t), [yc], d_y[YO.i])
                yo.free = [t]
                if j == NJ - 1:
                    tok["done", L, c] = [(s, s.n) for s in d_y]

            N = len(seq)
            for n in range(2):
                load(n)
            which(0)
            for n in range(N + 2):
                if n + 2 < N:
                    load(n + 2)
                hold = {}
                if 1 <= n < N + 1:
                    high(n - 1)
                if n < N:
                    up_a(n, hold)
                if 1 <= n < N + 1:
                    low(n - 1)
                side.step()
                if n < N:
                    up_b(n, hold)
                if n < N:
                    gate(n, hold)
                side.step()
                if n + 1 < N:
                    which(n + 1)
                if n >= 2:
                    down(n - 2)
                side.step()

        def combine(L, c, t0):
            def fetch(tile):
                yg = YG.next()
                for k in range(2):
                    t = pool(lambda e, k=k: e.indirect_dma_start(
                        yg.t[:, k, :], None, ys_d[L][c],
                        bass.IndirectOffsetOnAxis(ap=POSY[:, L, k, tile:tile + 1], axis=0)),
                        tok["done", L, c] + [tok["ypos", L, c]] + yg.free, d_g[YG.i])
                return yg, t

            def add(tile, f):
                yg, t = f
                a = t
                for k in range(2):
                    a = dve(lambda e, k=k: e.scalar_tensor_tensor(
                        out=X[:, tile, :], in0=yg.t[:, k, :], scalar=CW[:, L, k, tile:tile + 1],
                        in1=X[:, tile, :], op0=ALU.mult, op1=ALU.add), [t, a], s_x)
                yg.free = [a]
                x_ready[tile] = a

            got = {}
            for i in range(6):
                if i >= 2:
                    add(t0 + i - 2, got[i - 2])
                if i < 4:
                    got[i] = fetch(t0 + i)
                yield from gap(4 if i % 2 else 1)

        def attend(b, r, tr, spawn):
            hp, s16, hl_t, hta = r.hp, r.s16, r.hl_t, HTA
            k_s, k_all = tok["ks"], tok["kk"]
            H = hta.t
            yield from gap(2)
            for j in range(4):
                at_t = sp(lambda e, j=j: e.dma_start(H[:, :, 128 * j:128 * j + 128], s16.t[:, j, :], transpose=True),
                          [hl_t[j]] + hta.free, d_h)
            yield from gap(5)
            hta.free = []
            for m, dst in ((0, QS), (1, KS)):
                yield from tr.take()
                n = 0
                for db in range(2):
                    for wl, hl in ((0, 0), (0, 1), (1, 0)):
                        a = pe(lambda e, db=db, wl=wl, hl=hl, n=n, m=m: e.matmul(
                            tr.t[0:96, :], WQ[:, db, wl, m, :], H[:, 2 * hl + db, :], start=n == 0, stop=n == 5),
                            [at_t, tok["wq"]] + tr.free, s_at if n == 5 else None)
                        n += 1
                a = act(lambda e, dst=dst: e.activation(dst.t[:], tr.t[0:96, :], ACT.Copy, scale=2.0 ** -18),
                        [a] + dst.free, s_ac)
                yield from gap(2)
                lo = slice(64, 96) if m == 0 else slice(32, 64)
                a = dve(lambda e, dst=dst, lo=lo: e.scalar_tensor_tensor(
                    out=dst.t[lo, :], in0=tr.t[lo, :], scalar=2.0 ** -18, in1=dst.t[lo, :],
                    op0=ALU.mult, op1=ALU.subtract), [a], s_top)
                tr.give([a])
                dst.free = []
                qk_t = a
                yield from gap(1)

            def row(i):
                n = 128 * (i + 1)
                bs, bq = B[5], B[6]
                yield from bs.take()
                yield from bq.take()
                k = 0
                for db in range(2):
                    for l, rr in ((0, 0), (0, 1), (1, 0)):
                        pe(lambda e, db=db, l=l, rr=rr, k=k: e.matmul(
                            bs.t[:, 0:n], H[:, 2 * l + db, 128 * i:128 * i + 128], H[:, 2 * rr + db, 0:n],
                            start=k == 0, stop=False), [at_t] + bs.free)
                        k += 1
                a = pe(lambda e: e.matmul(bs.t[:, n - 128:n], identb[:], maskb[:], start=False, stop=True), [kd], s_sim)
                q = pe(lambda e: e.matmul(bq.t[:, 0:n], QS.t[:, 128 * i:128 * i + 128], KS.t[:, 0:n],
                                          start=True, stop=True), [qk_t] + bq.free, s_sco)
                if i == 3:
                    QS.free, KS.free, hta.free = [q], [q], [q]
                    tok["head", b] = True
                yield from gap(2)
                sm, at = SIM.next(), AT.next()
                m = dve(lambda e: e.max(at.t[:, 0:8], bs.t[:, 0:n]), [a] + at.free, s_top)
                m = dve(lambda e: e.match_replace(sm.t[:, 0:n], at.t[:, 0:8], bs.t[:, 0:n], MARK),
                        [m] + sm.free, s_top)
                bs.give([m])
                yield from gap(2)
                m = dve(lambda e: e.tensor_scalar(sm.t[:, 0:n], sm.t[:, 0:n], MARK, NEG, ALU.not_equal, ALU.mult),
                        [m], s_top)
                if i == 0:
                    m = dve(lambda e: e.tensor_tensor(sm.t[:, 0:128], sm.t[:, 0:128], maskf[:], ALU.min), [m], s_top)
                m = dve(lambda e: e.tensor_tensor_reduce(sm.t[:, 0:n], bq.t[:, 0:n], sm.t[:, 0:n], 1.0, -3e38,
                                                         ALU.add, ALU.max, at.t[:, 8:9]), [m, q], s_top)
                bq.give([m])
                m = dve(lambda e: e.tensor_scalar(at.t[:, 9:10], at.t[:, 8:9], K[:, 3:4], None, ALU.mult),
                        [m, k_all], s_top)
                yield from gap(1)
                p = act(lambda e: e.activation(sm.t[:, 0:n], sm.t[:, 0:n], ACT.Exp, bias=at.t[:, 9:10],
                                               scale=K[:, 2:3], accum_out=at.t[:, 10:11]), [m], s_p)
                hm = act(lambda e: e.activation(hp.t[:, i, :], hp.t[:, i, :], ACT.Copy, scale=k_mix[:, 0:1]),
                         [hl_t[-1], k_s], s_ac)
                yield from gap(3)
                yield from tr.take()
                for s in range(i + 1):
                    a = pe(lambda e, s=s: e.transpose(tr.t[:, 128 * s:128 * s + 128],
                                                      sm.t[:, 128 * s:128 * s + 128], identf[:]),
                           [p] + tr.free, s_pt if s == i else None)
                sm.free = [a]
                yield from gap(3)
                rr = p
                ph, ms = PH.next(), B[6]
                a = dve(lambda e: e.tensor_scalar(ph.t[:, 0, 0:n], tr.t[:, 0:n], 0.0, 2.0 ** 14, ALU.max, ALU.mult),
                        [a] + ph.free, s_ps)
                a = dve(lambda e: e.scalar_tensor_tensor(
                    out=ph.t[:, 1, 0:n], in0=tr.t[:, 0:n], scalar=2.0 ** 14, in1=ph.t[:, 0, 0:n],
                    op0=ALU.mult, op1=ALU.subtract), [a], s_ps)
                tr.give([a])
                if i == 0:
                    rr = dve(lambda e: e.tensor_tensor(at.t[:, 10:11], at.t[:, 10:11], extra0[:], ALU.add), [rr], s_top)
                rr = dve(lambda e: e.reciprocal(at.t[:, 11:12], at.t[:, 10:11]), [rr], s_top)
                rr = dve(lambda e: e.tensor_scalar(at.t[:, 12:13], at.t[:, 11:12], 0.0, 2.0 ** -24,
                                                   ALU.max, ALU.mult), [rr], s_top)
                rr = dve(lambda e: e.tensor_scalar(at.t[:, 13:14], at.t[:, 12:13], K[:, 5:6], None, ALU.mult),
                         [rr, k_s], s_top)
                yield from gap(2)
                yield from ms.take()
                terms = [(ph.t[:, l, 128 * s:128 * s + 128], s, r2) for s in range(i + 1)
                         for l, r2 in ((0, 0), (0, 1), (1, 0))]
                if i == 0:
                    terms += [(row0[:], s, r2) for s in range(1, 4) for r2 in range(2)]
                for z, (lhs, s, r2) in enumerate(terms):
                    last = z == len(terms) - 1
                    g = pe(lambda e, lhs=lhs, s=s, r2=r2, z=z, last=last: e.matmul(
                        ms.t[:, 0:256], lhs, s16.t[:, s, 256 * r2:256 * r2 + 256], start=z == 0, stop=last),
                        [a] + ms.free, s_msg if last else None)
                ph.free = [g]
                if i == 3:
                    s16.give([g])
                yield from gap(1)
                u = dve(lambda e: e.scalar_tensor_tensor(
                    out=hp.t[:, i, :], in0=ms.t[:, 0:256], scalar=at.t[:, 13:14], in1=hp.t[:, i, :],
                    op0=ALU.mult, op1=ALU.add), [g, hm, rr], s_bl)
                ms.give([u])
                at.free = [u]
                u = pool(lambda e: e.tensor_tensor(hp.t[:, i, :], hp.t[:, i, :], gain, ALU.mult),
                         [u, tok["gain"]], s_pb)
                bl.append(pool(lambda e: e.tensor_tensor(hp.t[:, i, :], hp.t[:, i, :], bias[:], ALU.add),
                               [u, ld_bi], s_pb))

            bl = []
            for i in range(4):
                spawn(row(i))
                yield from gap(ROWGAP)
            while len(bl) < 4:
                yield
            yield from gap(2)
            ge = act(lambda e: e.activation(hp.t[:], hp.t[:], ACT.Gelu), bl, s_gelu)
            yield from gap(2)
            for j in range(4):
                x_ready[4 * b + j] = dve(lambda e, j=j: e.scalar_tensor_tensor(
                    out=X[:, 4 * b + j, :], in0=hp.t[:, j, :], scalar=K[:, 6:7], in1=X[:, 4 * b + j, :],
                    op0=ALU.mult, op1=ALU.add), [ge], s_x)
            hp.give([x_ready[4 * b + 3]])
            tok["attended", b] = True

        class Side:
            def __init__(self):
                self.streams = []

            def step(self):
                for g in list(self.streams):
                    try:
                        next(g)
                    except StopIteration:
                        self.streams.remove(g)

            def finish(self):
                while self.streams:
                    self.step()

        recs = {}

        def attention_stream(c):
            for b in range(4 * c, 4 * c + 4):
                while ("normed", b) not in tok:
                    yield
                side.streams.append(attend(b, recs[b], B[0], spawn))
                while ("head", b) not in tok:
                    yield

        def prepare_stream(c):
            while ("done", 0, c) not in tok:
                yield
            for b in range(4 * c, 4 * c + 4):
                yield from combine(0, c, 4 * b)
                recs[b] = Rec()
                yield from norm(4 * b, recs[b])
                tok["normed", b] = True

        def router_stream(c):
            for g in range(NTC // 4):
                while ("attended", 4 * c + g) not in tok:
                    yield
                r = Rec()
                yield from gate_scores(c * NTC + 4 * g, r, B[7], B[3], 0, S16)
                yield from router(1, c, g, 4, B[3], [r])
            yield from tables(1, c, B[7])

        def final_stream(c):
            while ("done", 1, c) not in tok:
                yield
            for t0 in range(c * NTC, c * NTC + NTC, 4):
                yield from combine(1, c, t0)
                tok["out"] = sp(lambda e, t0=t0: e.dma_start(ov[:, t0:t0 + 4, :], X[:, t0:t0 + 4, :]),
                                [x_ready[t0 + 3]], d_o)

        k_mix = sb("k_mix", [128, 1], F32)
        tab_free = []
        mx = maxima()
        side = Side()
        def spawn(stream):
            side.streams.append(stream)

        def late():
            yield from gap(M0)
            yield from mx

        side.streams = [first_routers(0, [B[6], B[2]], [B[4], B[5], B[7], B[0]], spawn), late()]
        side.finish()
        rest = tables(0, 0, B[7])
        while ("table", 0, 0) not in tok:
            next(rest)
        parts_of_w = split()
        for _ in range(SPLIT):
            next(parts_of_w)
        split_qk()
        tok["ks"] = scalars()
        tok["ks"] = dve(lambda e: e.tensor_scalar(k_mix[:], K[:, 4:5], 2.0 ** -10, None, ALU.mult), [tok["ks"]], s_kd)

        def in_turn():
            yield from parts_of_w
            yield from rest
            tok["gain"] = sp(lambda e: e.dma_start(gain, gain_d), [tok["w"]], d_c[3])
            yield from first_routers(1, [B[6], B[0]], [B[7], B[5]], spawn)
            yield from tables(0, 1, B[7])
            for c in range(C):
                yield from router_stream(c)

        def prepares():
            for c in range(C):
                yield from prepare_stream(c)

        def attentions():
            for c in range(C):
                yield from attention_stream(c)

        def finals():
            for c in range(C):
                yield from final_stream(c)

        side.streams = [attentions(), in_turn(), prepares(), finals()]
        experts(side)
        side.finish()
        sp(lambda e: e.drain(), [tok["out"]] + [(s, s.n) for s in d_y] + z_rows)
        pool(lambda e: e.drain(), [(s, s.n) for s in d_sc] + [(d_pad, d_pad.n)])

        @block.sync
        def _(e):
            Q.emit("sync", e)

        @block.gpsimd
        def _(e):
            Q.emit("gpsimd", e)

        @block.scalar
        def _(e):
            Q.emit("scalar", e)

        @block.tensor
        def _(e):
            Q.emit("tensor", e)

        @block.vector
        def _(e):
            Q.emit("vector", e)


def program(nc, arrays):
    args = {}
    for name, a in arrays.items():
        args[name] = nc.dram_tensor(name, a.shape, mybir.dt.from_np(a.dtype), kind="ExternalInput").ap()
    out = nc.dram_tensor("out", (T, D), F32, kind="ExternalOutput").ap()
    hs = [[nc.dram_tensor(f"hs{l}{c}", (ROWS, 2 * D), F16, kind="Internal").ap() for c in range(C)] for l in range(2)]
    ys = [[nc.dram_tensor(f"ys{l}{c}", (NJ * 128, D), F32, kind="Internal").ap() for c in range(C)] for l in range(2)]
    macaron_kernel(nc, args["x"], args["wk"], args["wqk"], args["gw"], args["gain"], args["bias"], args["lg"],
                   out, hs, ys)


def layout(inputs):
    import numpy as np

    x = np.ascontiguousarray(np.asarray(inputs["L0_attn_x"]).reshape(T, D))
    w1 = np.asarray(inputs["L0_ffn_w1"]).transpose(0, 2, 1).reshape(NE, 2, 128, 512)
    w3 = np.asarray(inputs["L0_ffn_w3"]).transpose(0, 2, 1).reshape(NE, 2, 128, 512)
    w2 = np.asarray(inputs["L0_ffn_w2"]).transpose(0, 2, 1).reshape(NE, 4, 128, 256)
    up = np.concatenate([w1, w3], axis=3).transpose(2, 0, 1, 3).reshape(128, 16, 1024)
    down = w2.transpose(2, 0, 1, 3).reshape(128, 8, 1024)
    wk = np.ascontiguousarray(np.concatenate([up, down], axis=1))
    qk = np.concatenate([np.asarray(inputs["L0_attn_W_q"]), np.asarray(inputs["L0_attn_W_k"])], axis=0)
    wqk = np.ascontiguousarray(qk.T.reshape(2, 128, 64).transpose(1, 0, 2))
    gw = np.ascontiguousarray(np.asarray(inputs["L0_ffn_gate_w"]).T.reshape(2, 128, 8).transpose(1, 0, 2))
    gain = np.ascontiguousarray(np.broadcast_to(np.asarray(inputs["L0_attn_gain"])[None, :], (128, D)))
    bias = np.ascontiguousarray(np.broadcast_to(np.asarray(inputs["L0_attn_bias"])[None, :], (128, D)))
    lg = np.stack([np.asarray(inputs["L0_attn_log_mix"]), np.asarray(inputs["L0_attn_log_scale"])])
    lg = np.ascontiguousarray(np.broadcast_to(lg[None, :], (128, 2)))
    return {"x": x, "wk": wk, "wqk": wqk, "gw": gw, "gain": gain, "bias": bias, "lg": lg}


def kernel(**inputs):
    import concourse.bacc as bacc
    from concourse.bass_utils import run_bass_kernel_spmd

    nc = bacc.Bacc("TRN2", target_bir_lowering=False, num_devices=1)
    arrays = layout(inputs)
    program(nc, arrays)
    r = run_bass_kernel_spmd(nc, [arrays], core_ids=[0])
    return r.results[0]["out"].reshape(8, 512, D)
```
